# Optimizing a Trainium2 kernel written in Bass

```python
import numpy as np
import jax
import jax.numpy as jnp

def _softmax(x, axis=-1):
    return jax.nn.softmax(x, axis=axis)

def _gelu(x):
    return jax.nn.gelu(x, approximate=True)

def _silu(x):
    return jax.nn.silu(x)

def _sigmoid(x):
    return jax.nn.sigmoid(x)

def _layernorm(x, axis=-1, eps=1e-05):
    m = jnp.mean(x, axis=axis, keepdims=True)
    v = jnp.var(x, axis=axis, keepdims=True)
    return (x - m) / jnp.sqrt(v + eps)

def _scatter_add(tgt, idx, src, axis=0):
    return tgt.at[idx].add(src)

def _segment_sum(src, seg, n):
    return jax.ops.segment_sum(src, seg, n)
kernel_name = 'mk_gnn_ffn_d2_gnn_r16_b7a4e7'

def setup_inputs(seed: int=0):
    np.random.seed(seed)
    _w = jnp.asarray

    def _rec_inputs():
        import jax
        import jax.numpy as jnp
        _gk = jax.random.key(seed)
        x = -0.0003713 + 1 * jax.random.normal(jax.random.fold_in(_gk, 1), (6250, 256), jnp.float32)
        src = jax.random.randint(jax.random.fold_in(_gk, 2), (100000,), 0, 6250, jnp.int32)
        dst = jax.random.randint(jax.random.fold_in(_gk, 3), (100000,), 0, 6250, jnp.int32)
        _o = jnp.argsort(dst, stable=True)
        src = src[_o]
        dst = dst[_o]
        edge_attr_64 = -9.77346e-05 + 0.999888 * jax.random.normal(jax.random.fold_in(_gk, 12), (100000, 64), jnp.float32)
        return (x, src, dst, edge_attr_64)
    x, src, dst, edge_attr_64 = _rec_inputs()

    def _L0_gnn_setup():
        import jax, jax.numpy as jnp
        import numpy as np
        N_NODES = 3125
        N_EDGES = 50000
        IN_DIM = 256
        E_DIM = 64
        N_HEADS = 8
        OUT_DIM = 32
        NEG_SLOPE = 0.2
        key = jax.random.key(seed)
        ks = jax.random.split(key, 10)
        return {'feat': jax.random.normal(ks[0], (N_NODES, IN_DIM), dtype=jnp.float32), 'edge_attr': jax.random.normal(ks[1], (N_EDGES, E_DIM), dtype=jnp.float32), 'src': jax.random.randint(ks[2], (N_EDGES,), 0, N_NODES, dtype=jnp.int32), 'dst': jax.random.randint(ks[3], (N_EDGES,), 0, N_NODES, dtype=jnp.int32), 'W_fc': jax.random.normal(ks[4], (IN_DIM, N_HEADS * OUT_DIM), dtype=jnp.float32) * (1.0 / np.sqrt(IN_DIM)), 'W_e': jax.random.normal(ks[5], (E_DIM, N_HEADS * OUT_DIM), dtype=jnp.float32) * (1.0 / np.sqrt(E_DIM)), 'attn_h': jax.random.normal(ks[6], (N_HEADS, OUT_DIM), dtype=jnp.float32) * 0.1, 'attn_e': jax.random.normal(ks[7], (N_HEADS, OUT_DIM), dtype=jnp.float32) * 0.1, 'attn_t': jax.random.normal(ks[8], (N_HEADS, OUT_DIM), dtype=jnp.float32) * 0.1, 'bias': jnp.zeros((N_HEADS, OUT_DIM), dtype=jnp.float32)}
    _L0_gnn_all = _L0_gnn_setup()
    _L0_gnn_in = {k: v for k, v in _L0_gnn_all.items() if k in ('W_fc', 'W_e', 'attn_h', 'attn_e', 'attn_t', 'bias')}
    del _L0_gnn_all

    def _L0_ffn_setup():
        import jax, jax.numpy as jnp
        import numpy as np
        B, A = (256, 8)
        IN, OUT = (256, 256)
        SH1, SH2 = (256, 128)
        EH1, EH2 = (128, 64)
        E, TOPK = (4, 2)

        def _shared_mlp(x, W1, b1, W2, b2, W3, b3):
            h = jax.nn.relu(x @ W1 + b1)
            h = jax.nn.relu(h @ W2 + b2)
            return h @ W3 + b3

        def _experts_mlp(x, eW1, eb1, eW2, eb2, eW3, eb3):
            h = jax.nn.relu(jnp.einsum('baf,efh->ebah', x, eW1) + eb1[:, None, None, :])
            h = jax.nn.relu(jnp.einsum('ebah,ehg->ebag', h, eW2) + eb2[:, None, None, :])
            o = jnp.einsum('ebag,ego->ebao', h, eW3) + eb3[:, None, None, :]
            return jnp.moveaxis(o, 0, -1)
        key = jax.random.key(seed)
        ks = jax.random.split(key, 16)
        s = 0.05
        return {'x': jax.random.normal(ks[0], (B, A, IN), jnp.float32), 'sW1': jax.random.normal(ks[1], (IN, SH1), jnp.float32) * s, 'sb1': jnp.zeros((SH1,), jnp.float32), 'sW2': jax.random.normal(ks[2], (SH1, SH2), jnp.float32) * s, 'sb2': jnp.zeros((SH2,), jnp.float32), 'sW3': jax.random.normal(ks[3], (SH2, OUT), jnp.float32) * s, 'sb3': jnp.zeros((OUT,), jnp.float32), 'eW1': jax.random.normal(ks[4], (E, IN, EH1), jnp.float32) * s, 'eb1': jnp.zeros((E, EH1), jnp.float32), 'eW2': jax.random.normal(ks[5], (E, EH1, EH2), jnp.float32) * s, 'eb2': jnp.zeros((E, EH2), jnp.float32), 'eW3': jax.random.normal(ks[6], (E, EH2, OUT), jnp.float32) * s, 'eb3': jnp.zeros((E, OUT), jnp.float32), 'gW': jax.random.normal(ks[7], (IN, E), jnp.float32) * s, 'gb': jnp.zeros((E,), jnp.float32)}
    _L0_ffn_all = _L0_ffn_setup()
    _L0_ffn_in = {k: v for k, v in _L0_ffn_all.items() if k in ('sW1', 'sb1', 'sW2', 'sb2', 'sW3', 'sb3', 'eW1', 'eb1', 'eW2', 'eb2', 'eW3', 'eb3', 'gW', 'gb')}
    del _L0_ffn_all

    def _L1_gnn_setup():
        import jax, jax.numpy as jnp
        import numpy as np
        N_NODES = 4096
        N_EDGES = 65536
        HEADS = 4
        HEAD_DIM = 64
        DIM = 256
        BN_EPS = 1e-05
        key = jax.random.key(seed)
        k1, k2, k3, k4 = jax.random.split(key, 4)
        features = jax.random.normal(k1, (N_NODES, DIM), dtype=jnp.float32)
        src = jax.random.randint(k2, (N_EDGES,), 0, N_NODES, dtype=jnp.int64)
        dst = jax.random.randint(k3, (N_EDGES,), 0, N_NODES, dtype=jnp.int64)
        W_src = jax.random.normal(k4, (DIM, HEADS * HEAD_DIM), dtype=jnp.float32) * (1.0 / np.sqrt(DIM))
        gamma = jnp.ones((DIM,), dtype=jnp.float32)
        beta = jnp.zeros((DIM,), dtype=jnp.float32)
        return {'features': features, 'src': src, 'dst': dst, 'W_src': W_src, 'gamma': gamma, 'beta': beta}
    _L1_gnn_all = _L1_gnn_setup()
    _L1_gnn_in = {k: v for k, v in _L1_gnn_all.items() if k in ('W_src', 'gamma', 'beta')}
    del _L1_gnn_all

    def _L1_ffn_setup():
        import jax, jax.numpy as jnp
        import numpy as np
        B, K, D = (512, 16, 256)
        E = 32
        H = int(D * 0.25)
        key = jax.random.key(seed)
        ks = jax.random.split(key, 7)
        d_rs = D ** (-0.5)
        h_rs = H ** (-0.5)
        x = jax.random.normal(ks[0], (B, K, D), dtype=jnp.float32)
        router_w = jax.random.uniform(ks[1], (E, D), jnp.float32, -d_rs, d_rs)
        router_b = jax.random.uniform(ks[2], (E,), jnp.float32, -d_rs, d_rs)
        W1 = jax.random.uniform(ks[3], (E, D, H), jnp.float32, -h_rs, h_rs)
        b1 = jax.random.uniform(ks[4], (E, H), jnp.float32, -h_rs, h_rs)
        W2 = jax.random.uniform(ks[5], (E, H, D), jnp.float32, -d_rs, d_rs)
        b2 = jax.random.uniform(ks[6], (E, D), jnp.float32, -d_rs, d_rs)
        return {'x': x, 'router_w': router_w, 'router_b': router_b, 'W1': W1, 'b1': b1, 'W2': W2, 'b2': b2}
    _L1_ffn_all = _L1_ffn_setup()
    _L1_ffn_in = {k: v for k, v in _L1_ffn_all.items() if k in ('router_w', 'router_b', 'W1', 'b1', 'W2', 'b2')}
    del _L1_ffn_all
    return {'x': x, 'src': src, 'dst': dst, 'edge_attr_64': edge_attr_64, 'L0_gnn_W_fc': _L0_gnn_in['W_fc'], 'L0_gnn_W_e': _L0_gnn_in['W_e'], 'L0_gnn_attn_h': _L0_gnn_in['attn_h'], 'L0_gnn_attn_e': _L0_gnn_in['attn_e'], 'L0_gnn_attn_t': _L0_gnn_in['attn_t'], 'L0_gnn_bias': _L0_gnn_in['bias'], 'L0_ffn_sW1': _L0_ffn_in['sW1'], 'L0_ffn_sb1': _L0_ffn_in['sb1'], 'L0_ffn_sW2': _L0_ffn_in['sW2'], 'L0_ffn_sb2': _L0_ffn_in['sb2'], 'L0_ffn_sW3': _L0_ffn_in['sW3'], 'L0_ffn_sb3': _L0_ffn_in['sb3'], 'L0_ffn_eW1': _L0_ffn_in['eW1'], 'L0_ffn_eb1': _L0_ffn_in['eb1'], 'L0_ffn_eW2': _L0_ffn_in['eW2'], 'L0_ffn_eb2': _L0_ffn_in['eb2'], 'L0_ffn_eW3': _L0_ffn_in['eW3'], 'L0_ffn_eb3': _L0_ffn_in['eb3'], 'L0_ffn_gW': _L0_ffn_in['gW'], 'L0_ffn_gb': _L0_ffn_in['gb'], 'L1_gnn_W_src': _L1_gnn_in['W_src'], 'L1_gnn_gamma': _L1_gnn_in['gamma'], 'L1_gnn_beta': _L1_gnn_in['beta'], 'L1_ffn_router_w': _L1_ffn_in['router_w'], 'L1_ffn_router_b': _L1_ffn_in['router_b'], 'L1_ffn_W1': _L1_ffn_in['W1'], 'L1_ffn_b1': _L1_ffn_in['b1'], 'L1_ffn_W2': _L1_ffn_in['W2'], 'L1_ffn_b2': _L1_ffn_in['b2']}

def reference(x, src, dst, edge_attr_64, L0_gnn_W_fc, L0_gnn_W_e, L0_gnn_attn_h, L0_gnn_attn_e, L0_gnn_attn_t, L0_gnn_bias, L0_ffn_sW1, L0_ffn_sb1, L0_ffn_sW2, L0_ffn_sb2, L0_ffn_sW3, L0_ffn_sb3, L0_ffn_eW1, L0_ffn_eb1, L0_ffn_eW2, L0_ffn_eb2, L0_ffn_eW3, L0_ffn_eb3, L0_ffn_gW, L0_ffn_gb, L1_gnn_W_src, L1_gnn_gamma, L1_gnn_beta, L1_ffn_router_w, L1_ffn_router_b, L1_ffn_W1, L1_ffn_b1, L1_ffn_W2, L1_ffn_b2):
    import jax
    import jax.numpy as jnp

    def _L0_gnn_ref(feat, edge_attr, src, dst, W_fc, W_e, attn_h, attn_e, attn_t, bias):
        import jax, jax.numpy as jnp
        import numpy as np
        N_NODES = 3125
        N_EDGES = 50000
        IN_DIM = 256
        E_DIM = 64
        N_HEADS = 8
        OUT_DIM = 32
        NEG_SLOPE = 0.2
        N = feat.shape[0]
        H, D = attn_h.shape
        ft = (feat @ W_fc).reshape(N, H, D)
        eh = jnp.einsum('nhd,hd->nh', ft, attn_h)
        et = jnp.einsum('nhd,hd->nh', ft, attn_t)
        fe = (edge_attr @ W_e).reshape(-1, H, D)
        ee = jnp.einsum('ehd,hd->eh', fe, attn_e)
        e = jax.nn.leaky_relu(eh[src] + ee + et[dst], negative_slope=NEG_SLOPE)
        e_max = jax.ops.segment_max(e, dst, num_segments=N)
        e_max = jax.lax.stop_gradient(jnp.where(jnp.isfinite(e_max), e_max, 0.0))
        ex = jnp.exp(e - e_max[dst])
        denom = jax.ops.segment_sum(ex, dst, num_segments=N)
        a = ex / denom[dst]
        msg = ft[src] * a[:, :, None]
        rst = jax.ops.segment_sum(msg, dst, num_segments=N)
        rst = rst + bias[None, :, :]
        return rst.reshape(N, H * D)

    def _L0_ffn_ref(x, sW1, sb1, sW2, sb2, sW3, sb3, eW1, eb1, eW2, eb2, eW3, eb3, gW, gb):
        import jax, jax.numpy as jnp
        import numpy as np
        B, A = (256, 8)
        IN, OUT = (256, 256)
        SH1, SH2 = (256, 128)
        EH1, EH2 = (128, 64)
        E, TOPK = (4, 2)

        def _shared_mlp(x, W1, b1, W2, b2, W3, b3):
            h = jax.nn.relu(x @ W1 + b1)
            h = jax.nn.relu(h @ W2 + b2)
            return h @ W3 + b3

        def _experts_mlp(x, eW1, eb1, eW2, eb2, eW3, eb3):
            h = jax.nn.relu(jnp.einsum('baf,efh->ebah', x, eW1) + eb1[:, None, None, :])
            h = jax.nn.relu(jnp.einsum('ebah,ehg->ebag', h, eW2) + eb2[:, None, None, :])
            o = jnp.einsum('ebag,ego->ebao', h, eW3) + eb3[:, None, None, :]
            return jnp.moveaxis(o, 0, -1)
        all_out = _experts_mlp(x, eW1, eb1, eW2, eb2, eW3, eb3)
        shared = _shared_mlp(x, sW1, sb1, sW2, sb2, sW3, sb3)
        gates = jax.nn.softmax(x @ gW + gb, axis=-1)
        topv, topi = jax.lax.top_k(gates, TOPK)
        topw = jax.nn.softmax(topv, axis=-1)
        sel = jnp.take_along_axis(all_out, topi[:, :, None, :], axis=-1)
        gated = jnp.sum(sel * topw[:, :, None, :], axis=-1)
        return shared + gated

    def _L1_gnn_ref(features, src, dst, W_src, gamma, beta):
        import jax, jax.numpy as jnp
        import numpy as np
        N_NODES = 4096
        N_EDGES = 65536
        HEADS = 4
        HEAD_DIM = 64
        DIM = 256
        BN_EPS = 1e-05
        n = features.shape[0]
        feat_src = (features @ W_src).reshape(n, HEADS, HEAD_DIM)
        msgs = feat_src[src]
        sums = jax.ops.segment_sum(msgs, dst, num_segments=n)
        deg = jax.ops.segment_sum(jnp.ones((msgs.shape[0],), dtype=features.dtype), dst, num_segments=n)
        rst = sums / jnp.maximum(deg, 1.0)[:, None, None]
        rst = rst + features.reshape(n, HEADS, HEAD_DIM)
        x = rst.reshape(n, DIM)
        mean = jnp.mean(x, axis=0)
        var = jnp.mean(jnp.square(x - mean), axis=0)
        x = (x - mean) * jax.lax.rsqrt(var + BN_EPS) * gamma + beta
        return jax.nn.relu(x)

    def _L1_ffn_ref(x, router_w, router_b, W1, b1, W2, b2):
        import jax, jax.numpy as jnp
        import numpy as np
        B, K, D = (512, 16, 256)
        E = 32
        H = int(D * 0.25)
        xf = x.reshape(-1, D)
        logits = xf @ router_w.T + router_b
        idx = jnp.argmax(logits, axis=-1)
        w1t = jnp.take(W1, idx, axis=0)
        h = jnp.einsum('nd,ndh->nh', xf, w1t) + jnp.take(b1, idx, axis=0)
        h = jax.nn.relu(h)
        w2t = jnp.take(W2, idx, axis=0)
        out = jnp.einsum('nh,nhd->nd', h, w2t) + jnp.take(b2, idx, axis=0)
        out = jax.nn.relu(out)
        return out.reshape(x.shape)
    x = x + _L0_gnn_ref(_layernorm(x, axis=-1), edge_attr_64, src, dst, L0_gnn_W_fc, L0_gnn_W_e, L0_gnn_attn_h, L0_gnn_attn_e, L0_gnn_attn_t, L0_gnn_bias)
    x = x + _L0_ffn_ref(_layernorm(x, axis=-1)[None], L0_ffn_sW1, L0_ffn_sb1, L0_ffn_sW2, L0_ffn_sb2, L0_ffn_sW3, L0_ffn_sb3, L0_ffn_eW1, L0_ffn_eb1, L0_ffn_eW2, L0_ffn_eb2, L0_ffn_eW3, L0_ffn_eb3, L0_ffn_gW, L0_ffn_gb)[0]
    x = x + _L1_gnn_ref(_layernorm(x, axis=-1), src, dst, L1_gnn_W_src, L1_gnn_gamma, L1_gnn_beta)
    x = x + _L1_ffn_ref(_layernorm(x, axis=-1)[None], L1_ffn_router_w, L1_ffn_router_b, L1_ffn_W1, L1_ffn_b1, L1_ffn_W2, L1_ffn_b2)[0]
    return x

_drawn_inputs = setup_inputs


def setup_inputs(seed=0):
    import zlib

    import numpy as np

    out = dict(_drawn_inputs(seed))
    spreads = {'L0_gnn_bias': (0.0, 0.1),
     'L0_ffn_sb1': (0.0, 0.33),
     'L0_ffn_sb2': (0.0, 0.1),
     'L0_ffn_sb3': (0.0, 0.1),
     'L0_ffn_eb1': (0.0, 0.656),
     'L0_ffn_eb2': (0.0, 0.378),
     'L0_ffn_eb3': (0.0, 0.1),
     'L0_ffn_gb': (0.0, 0.327),
     'L1_gnn_gamma': (1.0, 0.2),
     'L1_gnn_beta': (0.0, 0.1)}
    factors = {'L1_ffn_b1': 8.0, 'L1_ffn_b2': 3.833}
    for name, (base, spread) in spreads.items():
        noise = np.random.default_rng([zlib.crc32(name.encode()), seed]).standard_normal(out[name].shape)
        drawn = base * np.exp(spread * noise) if base else spread * noise
        out[name] = jnp.asarray(drawn.astype(out[name].dtype))
    for name, factor in factors.items():
        out[name] = (out[name] * factor).astype(out[name].dtype)
    return out
```

```python
from contextlib import ExitStack, contextmanager

import concourse.bass as bass
from concourse import mybir

fp32 = mybir.dt.float32
bf16 = mybir.dt.bfloat16
i32 = mybir.dt.int32
u32 = mybir.dt.uint32
ALU = mybir.AluOpType
ACT = mybir.ActivationFunctionType
AX = mybir.AxisListType

P = 125
N, E, D = 6250, 100000, 256
NT = N // P
ES = E // P
KD = D // 128
H0, HD = 8, 32
DE = 64
NG, SH1, SH2, EH1, EH2 = 4, 256, 128, 128, 64
NE, EH = 32, 64
HB = NE * EH // 128
NR = N + P
QB = 100
EPS = 1e-5
SLOPE = 0.2
LOW = -1.0e30
SKIP = 4000000
GT = 2
GC = GT * P
ds = bass.ds


def hold(eng, sem, value, pace):
    eng.wait_ge(sem, value)
    eng.sem_inc(pace, 1)


def program(nc, x, src, dst, edge_attr, W_fc, W_e, attn_h, attn_e, attn_t, bias, sW1, sb1, sW2, sb2, sW3, sb3,
            eW1, eb1, eW2, eb2, eW3, eb3, gW, gb, W_src, gamma, beta, router_w, router_b, W1, b1, W2, b2, out):
    ctx = ExitStack()

    def dram(name, shape, dt=fp32):
        return nc.dram_tensor(name, shape, dt, kind="Internal").ap()

    FT = dram("ft_rows", (N, D))
    EHD = dram("eh_rows", (N, H0))
    ETD = dram("et_rows", (N, H0))
    STARTD = dram("et_at_starts", (E, H0))
    AD = dram("attention", (E, H0))
    RANKD = dram("edge_rank", (E,))
    RSUMD = dram("sums_by_rank", (N, D))
    XND = dram("normed_rows", (N, D))

    with ctx:
        def sb(stack, name, shape, dt=fp32):
            return stack.enter_context(nc.sbuf_tensor(name, shape, dt))

        def ps(stack, name, shape, dt=fp32):
            return stack.enter_context(nc.psum_tensor(name, shape, dt))

        current = []

        def sem(name):
            current[-1][1].append(current[-1][0].enter_context(nc.semaphore(name)))
            return current[-1][1][-1]

        def gather_sem(name):
            return ctx.enter_context(nc.semaphore(name))

        @contextmanager
        def phase():
            with ExitStack() as stack:
                current.append((stack, []))
                yield
                with nc.Block() as block:
                    @block.sync
                    def _(sp):
                        for one in current[-1][1]:
                            sp.sem_clear(one)
                current.pop()

        def sems(name, n):
            return [sem(f"{name}{k}") for k in range(n)]

        sem.gather = lambda name, n=1: [gather_sem(f"{name}{k}") for k in range(n)]

        pace = {e: ctx.enter_context(nc.semaphore(f"pace_{e}")) for e in ("pe", "act", "dve", "pool", "sp")}

        X = sb(ctx, "X", [P, NT * D])
        MEAN = sb(ctx, "MEAN", [P, NT])
        RSTD = sb(ctx, "RSTD", [P, NT])
        ident = sb(ctx, "ident", [128, 128])
        iota = sb(ctx, "iota", [128, 128])
        below = sb(ctx, "below", [128, 128])
        ones = sb(ctx, "ones", [1, 128])
        epsc = sb(ctx, "epsc", [128, 1])
        DEG = sb(ctx, "DEG", [P, NT])
        RDEG = sb(ctx, "RDEG", [P, NT])
        FIRSTI = sb(ctx, "FIRSTI", [P, NT], i32)
        RANKI = sb(ctx, "RANKI", [P, NT], i32)
        SRCT = sb(ctx, "SRCT", [P, ES], i32)
        RELT = sb(ctx, "RELT", [P, ES])
        BASEI = sb(ctx, "BASEI", [1, ES], i32)

        def xt(i):
            return X[:, ds(i * D, D)]

        with phase():
            constants(nc, sem, ident, iota, below, ones, epsc)
            embed_nodes(nc, sb, ps, sem, sems, pace, x, W_fc, attn_h, attn_t, X, MEAN, RSTD, ident, epsc,
                        FT, EHD, ETD)
        with phase():
            score_edges(nc, sb, ps, sem, sems, pace, src, dst, edge_attr, W_e, attn_e, ident, iota, below,
                        EHD, ETD, STARTD, AD, RANKD, DEG, RDEG, FIRSTI, RANKI, SRCT, RELT, BASEI)
        with phase(), ExitStack() as s:
            ACC = sb(s, "ACC0", [128, KD * NR])
            sum_segments(nc, sb, ps, sem, sems, pace, "a", FT, AD, iota, SRCT, RELT, BASEI, ACC)
            rank_rows(nc, sb, ps, sem, sems, pace, "a", ident, ACC, RSUMD)
        with phase():
            add_attention(nc, sb, sem, sems, pace, RSUMD, RANKI, bias, X)
            norm_stats(nc, sb, sem, "b", X, MEAN, RSTD, epsc)
            gated_experts(nc, sb, ps, sem, sems, pace, sW1, sb1, sW2, sb2, sW3, sb3, eW1, eb1, eW2, eb2, eW3, eb3,
                          gW, gb, X, MEAN, RSTD, ident, ones)
        with phase(), ExitStack() as s:
            norm_stats(nc, sb, sem, "c", X, MEAN, RSTD, epsc)
            store_normed(nc, sb, sem, sems, pace, X, MEAN, RSTD, XND)
            ACC = sb(s, "ACC1", [128, KD * NR])
            sum_segments(nc, sb, ps, sem, sems, pace, "b", XND, None, iota, SRCT, RELT, BASEI, ACC)
            rank_rows(nc, sb, ps, sem, sems, pace, "b", ident, ACC, RSUMD)
        with phase():
            mean_layer(nc, sb, ps, sem, sems, pace, RSUMD, RANKI, RDEG, W_src, gamma, beta, X, MEAN, RSTD, ident, epsc)
        with phase():
            norm_stats(nc, sb, sem, "d", X, MEAN, RSTD, epsc)
            top_experts(nc, sb, ps, sem, sems, pace, router_w, router_b, W1, b1, W2, b2, X, MEAN, RSTD,
                        ident, iota, ones, out)


def constants(nc, sem, ident, iota, below, ones, epsc):
    set0 = sem("const_set")
    with nc.Block() as block:
        @block.gpsimd
        def _(pool):
            nc.gpsimd.memset(ident[:, :], 0.0).then_inc(set0, 1)
            nc.gpsimd.memset(below[:, :], 1.0).then_inc(set0, 1)
            nc.gpsimd.memset(ones[:, :], 1.0)
            nc.gpsimd.memset(epsc[:, :], EPS)
            nc.gpsimd.iota(iota[:, :], pattern=[[1, 128]], base=0, channel_multiplier=0,
                           allow_small_or_imprecise_dtypes=True)
            pool.wait_ge(set0, 2)
            nc.gpsimd.affine_select(out=ident[:, :], in_=ident[:, :], compare_op=ALU.not_equal, fill=1.0,
                                    base=0, pattern=[[-1, 128]], channel_multiplier=1)
            nc.gpsimd.affine_select(out=below[:, :], in_=below[:, :], compare_op=ALU.is_gt, fill=0.0,
                                    base=0, pattern=[[1, 128]], channel_multiplier=-1)


def norm_stats(nc, sb, sem, tag, X, MEAN, RSTD, epsc):
    stats_done, sd_done = sem(f"stats_done_{tag}"), sem(f"sd_done_{tag}")
    with ExitStack() as s:
        ST = sb(s, f"ST{tag}", [P, NT * 6])
        MV = sb(s, f"MV{tag}", [P, NT, 2])
        SD = sb(s, f"SD{tag}", [P, NT])
        with nc.Block() as block:
            @block.vector
            def _(dve):
                with dve.Fori(0, NT // 2) as g:
                    for k in range(2):
                        nc.vector.bn_stats(ST[:, ds((g * 2 + k) * 6, 6)], X[:, ds((g * 2 + k) * D, D)])
                dve.drain()
                for i in range(NT):
                    nc.vector.bn_aggr(MV[:, i, :], ST[:, i * 6:i * 6 + 6])
                dve.drain()
                nc.vector.tensor_copy(MEAN[:, :], MV[:, :, 0]).then_inc(stats_done, 1)
                dve.wait_ge(sd_done, 1)
                nc.vector.reciprocal(RSTD[:, :], SD[:, :])

            @block.scalar
            def _(act):
                act.wait_ge(stats_done, 1)
                nc.scalar.activation(SD[:, :], MV[:, :, 1], ACT.Sqrt, bias=epsc[0:P, :]).then_inc(sd_done, 1)


def embed_nodes(nc, sb, ps, sem, sems, pace, x, W_fc, attn_h, attn_t, X, MEAN, RSTD, ident, epsc, FT, EHD, ETD):
    x_in, w_in = sem("x_in"), sem("w_in")
    with ExitStack() as s:
        W = sb(s, "Wext", [128, KD, D + 2 * H0])
        AH = sb(s, "AH", [128, D])
        AT = sb(s, "ATb", [128, D])
        TMP = sb(s, "Wtmp", [128, D])
        with nc.Block() as block:
            @block.sync
            def _(sp):
                sp.dma_start(W[:, :, 0:D], W_fc.rearrange("(k p) n -> p k n", p=128)).then_inc(w_in, 16)
                sp.dma_start(AH[:, :], attn_h.rearrange("h d -> (h d)").partition_broadcast(128)).then_inc(w_in, 16)
                sp.dma_start(AT[:, :], attn_t.rearrange("h d -> (h d)").partition_broadcast(128)).then_inc(w_in, 16)
                xv = x.rearrange("(p i) d -> p (i d)", i=NT)
                sp.dma_start(X[0:112, :], xv[0:112, :], max_dma_last_dim=4096).then_inc(x_in, 16)
                sp.dma_start(X[112:P, :], xv[112:P, :], max_dma_last_dim=4096).then_inc(x_in, 16)
                sp.wait_ge(w_in, 48)
                sp.wait_ge(x_in, 32)

            @block.vector
            def _(dve):
                dve.wait_ge(w_in, 48)
                for n, a in enumerate((AH, AT)):
                    for k in range(KD):
                        nc.vector.tensor_tensor(TMP[:, :], W[:, k, 0:D], a[:, :], ALU.mult)
                        dve.drain()
                        nc.vector.tensor_reduce(W[:, k, D + n * H0:D + (n + 1) * H0],
                                                TMP[:, :].rearrange("p (h d) -> p h d", d=HD), AX.X, ALU.add)
                        dve.drain()
        norm_stats(nc, sb, sem, "a", X, MEAN, RSTD, epsc)

        WX = D + 2 * H0
        xn = [sb(s, f"xn{k}", [P, D]) for k in range(GT)]
        xnT = [sb(s, f"xnT{k}", [128, KD * P]) for k in range(GT)]
        row = [sb(s, f"row{k}", [P, WX]) for k in range(GT)]
        pT = [ps(s, f"pT{k}", [128, 512]) for k in range(GT)]
        pF = [ps(s, f"pF{k}", [128, 512]) for k in range(GT)]
        xn_ready, xn_free = sems("xn_ready", GT), sems("xn_free", GT)
        t_ready, xT_ready, xT_free = sems("t_ready", GT), sems("xT_ready", GT), sems("xT_free", GT)
        f_ready, row_ready, row_free = sems("f_ready", GT), sems("row_ready", GT), sems("row_free", GT)
        stored = sems("row_stored", GT)
        ftv = FT.rearrange("(p i) d -> p i d", i=NT)
        ehv = EHD.rearrange("(p i) d -> p i d", i=NT)
        etv = ETD.rearrange("(p i) d -> p i d", i=NT)
        with nc.Block() as block:
            @block.vector
            def _(dve):
                with dve.Fori(0, NT // GT) as g:
                    for k in range(GT):
                        hold(dve, xn_free[k], g + 1, pace["dve"])
                        i = g * GT + k
                        nc.vector.tensor_scalar(xn[k][:, :], X[:, ds(i * D, D)], MEAN[:, ds(i, 1)],
                                                RSTD[:, ds(i, 1)], ALU.subtract, ALU.mult).then_inc(xn_ready[k], 1)

            @block.tensor
            def _(pe):
                for k in range(GT):
                    pe.sem_inc(xn_free[k], 1)
                    pe.sem_inc(xT_free[k], 1)
                with pe.Fori(0, NT // GT) as g:
                    for k in range(GT):
                        hold(pe, xn_ready[k], g + 1, pace["pe"])
                        nc.tensor.transpose(pT[k][:, 0:P], xn[k][:, 0:128], ident[0:P, 0:P])
                        nc.tensor.transpose(pT[k][:, P:2 * P], xn[k][:, 128:D], ident[0:P, 0:P]).then_inc(t_ready[k], 1)
                        pe.sem_inc(pace["pe"], 1)
                    for k in range(GT):
                        hold(pe, xT_ready[k], g + 1, pace["pe"])
                        pe.sem_inc(xn_free[k], 1)
                        hold(pe, row_free[k], g + 1, pace["pe"])
                        for c in range(KD):
                            last = nc.tensor.matmul(pF[k][0:P, 0:WX], xnT[k][:, c * P:(c + 1) * P], W[:, c, :],
                                                    start=(c == 0), stop=(c == KD - 1))
                        last.then_inc(f_ready[k], 1)

            @block.scalar
            def _(act):
                for k in range(GT):
                    act.sem_inc(row_free[k], 1)
                with act.Fori(0, NT // GT) as g:
                    for k in range(GT):
                        hold(act, t_ready[k], g + 1, pace["act"])
                        nc.scalar.activation(xnT[k][:, :], pT[k][:, 0:2 * P], ACT.Copy).then_inc(xT_ready[k], 1)
                    for k in range(GT):
                        hold(act, f_ready[k], g + 1, pace["act"])
                        hold(act, stored[k], g * 48 + 48, pace["act"])
                        nc.scalar.activation(row[k][:, :], pF[k][0:P, 0:WX], ACT.Copy).then_inc(row_ready[k], 1)
                        hold(act, row_ready[k], g + 1, pace["act"])
                        act.sem_inc(row_free[k], 1)

            @block.sync
            def _(sp):
                for k in range(GT):
                    sp.sem_inc(stored[k], 48)
                with sp.Fori(0, NT // GT) as g:
                    for k in range(GT):
                        hold(sp, row_ready[k], g + 1, pace["sp"])
                        i = g * GT + k
                        for to, a, b in ((ftv, 0, D), (ehv, D, D + H0), (etv, D + H0, WX)):
                            sp.dma_start(to[:, ds(i, 1), :].rearrange("p o d -> p (o d)"),
                                         row[k][:, a:b]).then_inc(stored[k], 16)
                for k in range(GT):
                    sp.wait_ge(stored[k], 48 * (NT // GT + 1))


def score_edges(nc, sb, ps, sem, sems, pace, src, dst, edge_attr, W_e, attn_e, ident, iota, below,
                EHD, ETD, STARTD, AD, RANKD, DEG, RDEG, FIRSTI, RANKI, SRCT, RELT, BASEI):
    C = 16
    NCH = ES // C
    with ExitStack() as s:
        V = sb(s, "V", [P, ES * H0])
        F = sb(s, "F", [P, ES * H0])
        DX = sb(s, "DX", [P, ES + 2])
        DXI = sb(s, "DXI", [P, ES + 2], i32)
        SRCS = sb(s, "SRCS", [P, ES], i32)
        ZB = sb(s, "ZB", [128, 128], bf16)
        with ExitStack() as t:
            QI = sb(t, "QI", [QB, ES // QB, P], i32)
            QF = sb(t, "QF", [QB, ES // QB, P])
            ebuf = [sb(t, f"ebuf{k}", [P, C * DE]) for k in range(2)]
            eT = [sb(t, f"eT{k}", [128, C // 2 * P]) for k in range(2)]
            ehs = [sb(t, f"ehs{k}", [P, C * H0]) for k in range(2)]
            idx = [sb(t, f"idx{k}", [P, C], i32) for k in range(2)]
            hotA = [sb(t, f"hotA{k}", [P, C, P], bf16) for k in range(2)]
            hotB = [sb(t, f"hotB{k}", [P, C, NT], bf16) for k in range(2)]
            DA = sb(t, "DA", [P, ES])
            DB = sb(t, "DB", [P, ES])
            WE = sb(t, "WE", [128, D])
            AE = sb(t, "AE", [128, D])
            VB = sb(t, "VB", [128, 2 * H0])
            pQ = ps(t, "pQ", [128, 512])
            pE = [ps(t, f"pE{k}", [128, 512]) for k in range(2)]
            pX = [ps(t, f"pX{k}", [128, 512]) for k in range(2)]
            pS = [ps(t, f"pS{k}", [128, 512]) for k in range(2)]
            pH = ps(t, "pH", [128, 512])

            ld, wld, prep, qt, qc = sem("idx_in"), sem("we_in"), sem("idx_prep"), sem("q_transposed"), sem("q_copied")
            zero_in = sem("starts_zeroed")
            with nc.Block() as block:
                @block.sync
                def _(sp):
                    sv, dv = (a.rearrange("(p j) -> p j", j=ES) for a in (src, dst))
                    sp.dma_start(SRCS[:, :], sv).then_inc(ld, 16)
                    sp.dma_start(DXI[:, 1:ES + 1], dv).then_inc(ld, 16)
                    sp.dma_start(QI[:, :, :], src.rearrange("(b q p) -> q b p", q=QB, p=P)).then_inc(ld, 16)
                    sp.wait_ge(prep, 1)
                    sp.dma_start(DXI[1:P, 0:1], dv[0:P - 1, ES - 1:ES], allow_slow_non_contiguous=True).then_inc(ld, 16)
                    sp.dma_start(DXI[0:P - 1, ES + 1:ES + 2], dv[1:P, 0:1], allow_slow_non_contiguous=True).then_inc(ld, 16)
                    for k in range(2):
                        sp.dma_start(WE[k * DE:(k + 1) * DE, :], W_e[:, :]).then_inc(wld, 16)
                    sp.dma_start(AE[:, :], attn_e.rearrange("h d -> (h d)").partition_broadcast(128)).then_inc(wld, 16)
                    sp.dma_start(STARTD.rearrange("(p j) h -> p (j h)", j=ES), F[:, :]).then_inc(zero_in, 16)
                    sp.wait_ge(zero_in, 16)

                @block.vector
                def _(dve):
                    nc.vector.memset(DXI[:, 0:1], -1)
                    nc.vector.memset(DXI[:, ES + 1:ES + 2], -2)
                    nc.vector.memset(F[:, :], 0.0).then_inc(prep, 1)
                    nc.vector.memset(VB[:, :], 0.0)
                    nc.vector.memset(ZB[:, :], 0.0)
                    dve.wait_ge(ld, 80)
                    nc.vector.tensor_copy(QF[:, :, :], QI[:, :, :]).then_inc(prep, 1)
                    nc.vector.tensor_copy(DX[:, :], DXI[:, :])
                    dve.drain()
                    nc.vector.tensor_scalar(DB[:, :], DX[:, 1:ES + 1], (NT - 1) / 2.0, 1.0 / NT, ALU.subtract, ALU.mult)
                    dve.drain()
                    nc.vector.tensor_scalar(DB[:, :], DB[:, :], 12582912.0, None, ALU.add)
                    dve.drain()
                    nc.vector.tensor_scalar(DA[:, :], DB[:, :], 12582912.0, None, ALU.subtract)
                    dve.drain()
                    nc.vector.scalar_tensor_tensor(DB[:, :], DA[:, :], -float(NT), DX[:, 1:ES + 1], ALU.mult, ALU.add)
                    dve.wait_ge(wld, 48)
                    nc.vector.tensor_tensor(WE[:, :], WE[:, :], AE[:, :], ALU.mult)
                    dve.drain()
                    for k in range(2):
                        a = slice(k * DE, (k + 1) * DE)
                        nc.vector.tensor_reduce(VB[a, k * H0:(k + 1) * H0],
                                                WE[a, :].rearrange("p (h d) -> p h d", d=HD), AX.X, ALU.add)
                    for b in range(ES // QB):
                        dve.wait_ge(qt, b + 1)
                        nc.vector.tensor_copy(SRCT[:, b * QB:(b + 1) * QB], pQ[0:P, 0:QB]).then_inc(qc, 1)

                @block.tensor
                def _(pe):
                    pe.wait_ge(prep, 2)
                    for b in range(ES // QB):
                        if b:
                            pe.wait_ge(qc, b)
                        nc.tensor.transpose(pQ[0:P, 0:QB], QF[:, b, :], ident[0:QB, 0:QB]).then_inc(qt, 1)

            e_in, e_free = sems("attr_in", 2), sems("attr_free", 2)
            g_in, g_free = sem.gather("eh_in", 2), sems("eh_free", 2)
            idx_ready = sems("idx_ready", 2)
            tr, cp = sems("attr_T", 2), sems("attr_Tcopied", 2)
            sc, sc_free = sems("edge_scores", 2), sems("edge_scores_free", 2)
            hot, hot_free = sems("hot", 2), sems("hot_free", 2)
            ev = edge_attr.rearrange("(p j) d -> p (j d)", j=ES)
            with nc.Block() as block:
                @block.gpsimd
                def _(pool):
                    with pool.Fori(0, NCH // 2) as g:
                        for k in range(2):
                            hold(pool, g_free[k], g + 1, pace["pool"])
                            nc.gpsimd.tensor_copy(idx[k][:, :], SRCS[:, ds((g * 2 + k) * C, C)])
                            pool.drain()
                            for m in range(C):
                                pool.indirect_dma_start(ehs[k][:, m * H0:(m + 1) * H0], None, EHD[:, :],
                                                        bass.IndirectOffsetOnAxis(ap=idx[k][:, m:m + 1], axis=0)
                                                        ).then_inc(g_in[k], 16)

                @block.sync
                def _(sp):
                    with sp.Fori(0, NCH // 2) as g:
                        for k in range(2):
                            hold(sp, e_free[k], g + 1, pace["sp"])
                            j = (g * 2 + k) * (C * DE)
                            sp.dma_start(ebuf[k][:, :], ev[:, ds(j, C * DE)]).then_inc(e_in[k], 16)

                @block.tensor
                def _(pe):
                    for k in range(2):
                        pe.sem_inc(e_free[k], 1)
                        pe.sem_inc(hot_free[k], 1)
                    nc.tensor.matmul(pH[0:P, 0:NT], ZB[0:P, 0:P], ZB[0:P, 0:NT], start=True, stop=False,
                                     skip_group_check=True)
                    with pe.Fori(0, NCH // 2) as g:
                        for k in range(2):
                            hold(pe, e_in[k], g * 16 + 16, pace["pe"])
                            for m in range(C // 2):
                                to = (pE, pX)[m // 4][k]
                                last = nc.tensor.transpose(to[:, (m % 4) * P:(m % 4 + 1) * P],
                                                           ebuf[k][:, m * 2 * DE:(m + 1) * 2 * DE], ident[0:P, 0:P])
                            last.then_inc(tr[k], 1)
                            hold(pe, hot[k], g + 1, pace["pe"])
                            for m in range(C):
                                last = nc.tensor.matmul(pH[0:P, 0:NT], hotA[k][:, m, :], hotB[k][:, m, :],
                                                        start=False, stop=False, skip_group_check=True)
                            last.then_inc(hot_free[k], 1)
                            hold(pe, cp[k], g + 1, pace["pe"])
                            pe.sem_inc(e_free[k], 1)
                            hold(pe, sc_free[k], g + 1, pace["pe"])
                            for m in range(C // 2):
                                last = nc.tensor.matmul(pS[k][0:P, m * 2 * H0:(m + 1) * 2 * H0],
                                                        eT[k][:, m * P:(m + 1) * P], VB[:, :], start=True, stop=True)
                            last.then_inc(sc[k], 1)
                    nc.tensor.matmul(pH[0:P, 0:NT], ZB[0:P, 0:P], ZB[0:P, 0:NT], start=False, stop=True,
                                     skip_group_check=True)

                @block.scalar
                def _(act):
                    with act.Fori(0, NCH // 2) as g:
                        for k in range(2):
                            hold(act, tr[k], g + 1, pace["act"])
                            hold(act, sc_free[k], g + 1, pace["act"])
                            nc.scalar.activation(eT[k][:, 0:4 * P], pE[k][:, 0:4 * P], ACT.Copy)
                            nc.scalar.activation(eT[k][:, 4 * P:8 * P], pX[k][:, 0:4 * P], ACT.Copy).then_inc(cp[k], 1)

                @block.vector
                def _(dve):
                    for k in range(2):
                        dve.sem_inc(g_free[k], 1)
                        dve.sem_inc(sc_free[k], 1)
                    with dve.Fori(0, NCH // 2) as g:
                        for k in range(2):
                            j = (g * 2 + k) * C
                            hold(dve, hot_free[k], g + 1, pace["dve"])
                            for to, a, w in ((hotA, DA, P), (hotB, DB, NT)):
                                last = nc.vector.tensor_tensor(
                                    to[k][:, :, :], iota[0:P, 0:w].unsqueeze(1).to_broadcast([P, C, w]),
                                    a[:, ds(j, C)].unsqueeze(2).to_broadcast([P, C, w]), ALU.is_equal)
                            last.then_inc(hot[k], 1)
                            hold(dve, sc[k], g + 1, pace["dve"])
                            hold(dve, g_in[k], g * (16 * C) + 16 * C, pace["dve"])
                            nc.vector.tensor_tensor(V[:, ds(j * H0, C * H0)], pS[k][0:P, 0:C * H0], ehs[k][:, :],
                                                    ALU.add).then_inc(sc_free[k], 1)
                            hold(dve, sc_free[k], g + 2, pace["dve"])
                            dve.sem_inc(g_free[k], 1)

            tot, pre = sem("node_totals"), sem("node_prefix")
            INC = sb(t, "INC", [P, 2, NT])
            NEQ = sb(t, "NEQ", [P, NT])
            UN = sb(t, "UN", [P, NT])
            TOT = sb(t, "TOT", [P, 2])
            with nc.Block() as block:
                @block.vector
                def _(dve):
                    nc.vector.tensor_copy(DEG[:, :], pH[0:P, 0:NT])
                    nc.vector.memset(UN[:, :], 1.0)
                    dve.drain()
                    nc.vector.tensor_scalar(NEQ[:, :], DEG[:, :], 1.0, None, ALU.min)
                    nc.vector.tensor_scalar(RDEG[:, :], DEG[:, :], 1.0, None, ALU.max)
                    dve.drain()
                    nc.vector.reciprocal(RDEG[:, :], RDEG[:, :])
                    nc.vector.tensor_tensor_scan(INC[:, 0, :], UN[:, :], DEG[:, :], 0.0, ALU.mult, ALU.add)
                    nc.vector.tensor_tensor_scan(INC[:, 1, :], UN[:, :], NEQ[:, :], 0.0, ALU.mult, ALU.add)
                    dve.drain()
                    nc.vector.tensor_copy(TOT[:, :], INC[:, :, NT - 1]).then_inc(tot, 1)
                    dve.drain()
                    nc.vector.tensor_tensor(INC[:, 0, :], INC[:, 0, :], DEG[:, :], ALU.subtract)
                    nc.vector.tensor_tensor(INC[:, 1, :], INC[:, 1, :], NEQ[:, :], ALU.subtract)
                    nc.vector.tensor_scalar(UN[:, :], NEQ[:, :], 1.0, -float(SKIP), ALU.subtract, ALU.mult)
                    dve.drain()
                    dve.wait_ge(pre, 1)
                    for n, to in enumerate((FIRSTI, RANKI)):
                        nc.vector.scalar_tensor_tensor(to[:, :], INC[:, n, :], pQ[0:P, n:n + 1], UN[:, :], ALU.add, ALU.add)

                @block.tensor
                def _(pe):
                    pe.wait_ge(tot, 1)
                    for n in range(2):
                        last = nc.tensor.matmul(pQ[0:P, n:n + 1], below[0:P, 0:P], TOT[:, n:n + 1], start=True, stop=True)
                    last.then_inc(pre, 1)


        st_et = sem.gather("et_loaded")[0]
        with ExitStack() as t:
            ETS = sb(t, "ETS", [P, NT * H0])
            K = 10
            islot = [sb(t, f"islot{k}", [P, K], i32) for k in range(2)]
            eslot = [sb(t, f"eslot{k}", [P, K * H0]) for k in range(2)]
            st = sem.gather("starts", 2)
            with nc.Block() as block:
                @block.gpsimd
                def _(pool):
                    pool.dma_start(ETS[:, :], ETD.rearrange("(p i) h -> p (i h)", i=NT)).then_inc(st_et, 16)
                    pool.wait_ge(st_et, 16)
                    for n in range(NT // K):
                        k = n % 2
                        if n >= 2:
                            pool.wait_ge(st[k], 16 * K * (n // 2))
                        nc.gpsimd.tensor_copy(islot[k][:, :], FIRSTI[:, n * K:(n + 1) * K])
                        nc.gpsimd.tensor_copy(eslot[k][:, :], ETS[:, n * K * H0:(n + 1) * K * H0])
                        pool.drain()
                        for m in range(K):
                            pool.indirect_dma_start(STARTD[:, :], bass.IndirectOffsetOnAxis(ap=islot[k][:, m:m + 1], axis=0),
                                                    eslot[k][:, m * H0:(m + 1) * H0], None,
                                                    bounds_check=E - 1, oob_is_err=False).then_inc(st[k], 16)
                    for k in range(2):
                        pool.wait_ge(st[k], 16 * K * ((NT // K + 1 - k) // 2))

        with ExitStack() as t:
            B = sb(t, "B", [P, ES * H0])
            CONT = sb(t, "CONT", [P, ES + 1])
            PEN = sb(t, "PEN", [P, ES + 1])
            RK = sb(t, "RK", [P, ES])
            ONE = sb(t, "ONE", [P, ES])
            C0 = sb(t, "C0", [P, H0])
            ALLC = sb(t, "ALLC", [P, 2, H0])
            ENDS = sb(t, "ENDS", [P, 2, H0])
            CH = sb(t, "CH", [H0, 4 * P])
            CP = sb(t, "CP", [H0, 2 * P])
            CARRY = sb(t, "CARRY", [H0, 2, P + 1])
            CIN = sb(t, "CIN", [P, 2, H0])
            OFF = sb(t, "OFF", [P, 1])
            TOTR = sb(t, "TOTR", [P, 1])
            RQ = sb(t, "RQ", [QB, ES // QB, P])
            OFFQ = sb(t, "OFFQ", [QB, ES // QB])
            BASEF = sb(t, "BASEF", [1, ES])
            pC = ps(t, "pC", [128, 512])
            pB = ps(t, "pB", [128, 512])
            pR = [ps(t, f"pR{k}", [128, 512]) for k in range(2)]
            in_, c0_in, m_done, ex_done = sem("starts_in"), sem.gather("c0_in")[0], sem("max_done"), sem("exp_done")
            ends, chain, carr, cin = sem("ends"), sem("chain"), sem("carries"), sem("carries_in")
            rtot, rpre, rk_done = sem("rank_totals"), sem("rank_prefix"), sem("ranks_done")
            rk_out, rq_in, rq_done, rt, rtc = (sem("ranks_out"), sem("ranks_in"), sem("ranks_rel"), sem("ranks_T"),
                                               sem("ranks_Tcopied"))
            a_done, a_out = sem("attn_done"), sem("attn_out")

            def head(buf, h, back=False):
                v = buf[:, :].rearrange("p (j h) -> p j h", h=H0)[:, :, h]
                return v[:, ::-1] if back else v

            with nc.Block() as block:
                @block.gpsimd
                def _(pool):
                    pool.indirect_dma_start(C0[:, :], None, ETD[:, :],
                                            bass.IndirectOffsetOnAxis(ap=DXI[:, 1:2], axis=0)).then_inc(c0_in, 16)

                @block.sync
                def _(sp):
                    sp.dma_start(F[:, :], STARTD.rearrange("(p j) h -> p (j h)", j=ES)).then_inc(in_, 16)
                    sp.wait_ge(rk_done, 1)
                    sp.dma_start(RANKD.rearrange("(p j) -> p j", j=ES), RK[:, :]).then_inc(rk_out, 16)
                    sp.wait_ge(rk_out, 16)
                    sp.dma_start(RQ[:, :, :], RANKD.rearrange("(b q p) -> q b p", q=QB, p=P)).then_inc(rq_in, 16)
                    sp.dma_start(BASEF[:, :], RANKD.rearrange("(o t p) -> o t p", o=1, p=P)[:, :, 0],
                                 allow_slow_non_contiguous=True).then_inc(rq_in, 16)
                    sp.wait_ge(a_done, 1)
                    sp.dma_start(AD.rearrange("(p j) h -> p (j h)", j=ES), V[:, :]).then_inc(a_out, 16)
                    sp.wait_ge(a_out, 16)

                @block.scalar
                def _(act):
                    act.wait_ge(m_done, 1)
                    nc.scalar.activation(V[:, :], V[:, :], ACT.Exp).then_inc(ex_done, 1)

                @block.tensor
                def _(pe):
                    pe.wait_ge(rtot, 1)
                    nc.tensor.matmul(pR[0][0:P, 0:1], below[0:P, 0:P], TOTR[:, :], start=True, stop=True).then_inc(rpre, 1)
                    for n in range(2):
                        pe.wait_ge(ends, n + 1)
                        for c, v in enumerate((ENDS[:, 0, :], ENDS[:, 1, :], ALLC[:, 0, :], ALLC[:, 1, :])):
                            last = nc.tensor.transpose(pC[0:H0, c * P:(c + 1) * P], v, ident[0:P, 0:P])
                        last.then_inc(chain, 1)
                        pe.wait_ge(carr, n + 1)
                        nc.tensor.transpose(pB[0:P, 0:H0], CARRY[:, 0, 0:P], ident[0:H0, 0:H0])
                        nc.tensor.transpose(pB[0:P, H0:2 * H0], CARRY[:, 1, 1:P + 1], ident[0:H0, 0:H0]).then_inc(cin, 1)
                    for b in range(ES // QB):
                        pe.wait_ge(rq_done, 1)
                        if b >= 2:
                            pe.wait_ge(rtc, b - 1)
                        nc.tensor.transpose(pR[b % 2][0:P, 0:QB], RQ[:, b, :], ident[0:QB, 0:QB]).then_inc(rt, 1)

                @block.vector
                def _(dve):
                    nc.vector.tensor_tensor(CONT[:, :], DX[:, 1:ES + 2], DX[:, 0:ES + 1], ALU.is_equal)
                    nc.vector.memset(ONE[:, :], 1.0)
                    dve.drain()
                    nc.vector.tensor_scalar(PEN[:, :], CONT[:, :], 1.0, -LOW, ALU.subtract, ALU.mult)
                    nc.vector.tensor_scalar(RK[:, :], CONT[:, 0:ES], -1.0, 1.0, ALU.mult, ALU.add)
                    for n in range(2):
                        nc.vector.tensor_reduce(OFF[:, :], CONT[:, n:n + ES], AX.X, ALU.min)
                        dve.drain()
                        nc.vector.tensor_copy(ALLC[:, n, :], OFF[:, 0:1].to_broadcast([P, H0]))
                        dve.drain()
                    nc.vector.tensor_tensor_scan(RK[:, :], ONE[:, :], RK[:, :], 0.0, ALU.mult, ALU.add)
                    dve.drain()
                    nc.vector.tensor_copy(TOTR[:, :], RK[:, ES - 1:ES]).then_inc(rtot, 1)
                    dve.wait_ge(rpre, 1)
                    nc.vector.tensor_scalar(OFF[:, :], pR[0][0:P, 0:1], 1.0, None, ALU.subtract)
                    dve.drain()
                    nc.vector.tensor_scalar(RK[:, :], RK[:, :], OFF[:, :], None, ALU.add).then_inc(rk_done, 1)
                    dve.wait_ge(in_, 16)
                    dve.wait_ge(c0_in, 16)
                    for h in range(H0):
                        nc.vector.tensor_tensor_scan(head(F, h), CONT[:, 0:ES], head(F, h), C0[:, h:h + 1], ALU.mult, ALU.add)
                    dve.drain()
                    nc.vector.tensor_tensor(V[:, :], V[:, :], F[:, :], ALU.add)
                    dve.drain()
                    nc.vector.scalar_tensor_tensor(V[:, :], V[:, :], SLOPE, V[:, :], ALU.mult, ALU.max)
                    dve.drain()
                    for n, (data, first, op0, op1) in enumerate(((PEN, LOW, ALU.add, ALU.max),
                                                                 (CONT, 0.0, ALU.mult, ALU.add))):
                        for r in range(2):
                            for h in range(H0):
                                f0 = first if r == 0 else CIN[:, 0, h:h + 1]
                                b0 = first if r == 0 else CIN[:, 1, h:h + 1]
                                nc.vector.tensor_tensor_scan(head(F, h), data[:, 0:ES], head(V, h), f0, op0, op1)
                                nc.vector.tensor_tensor_scan(head(B, h, True), data[:, 1:ES + 1][:, ::-1],
                                                             head(V, h, True), b0, op0, op1)
                            dve.drain()
                            if r:
                                continue
                            nc.vector.tensor_copy(ENDS[:, 0, :], F[:, (ES - 1) * H0:ES * H0])
                            nc.vector.tensor_copy(ENDS[:, 1, :], B[:, 0:H0]).then_inc(ends, 1)
                            dve.wait_ge(chain, n + 1)
                            nc.vector.tensor_copy(CH[:, :], pC[0:H0, 0:4 * P])
                            dve.drain()
                            if n == 0:
                                nc.vector.tensor_scalar(CP[:, :], CH[:, 2 * P:4 * P], 1.0, -LOW, ALU.subtract, ALU.mult)
                            else:
                                nc.vector.tensor_copy(CP[:, :], CH[:, 2 * P:4 * P])
                            nc.vector.memset(CARRY[:, 0, 0:1], first)
                            nc.vector.memset(CARRY[:, 1, P:P + 1], first)
                            dve.drain()
                            nc.vector.tensor_tensor_scan(CARRY[:, 0, 1:P + 1], CP[:, 0:P], CH[:, 0:P], first, op0, op1)
                            nc.vector.tensor_tensor_scan(CARRY[:, 1, 0:P][:, ::-1], CP[:, P:2 * P][:, ::-1],
                                                         CH[:, P:2 * P][:, ::-1], first, op0, op1).then_inc(carr, 1)
                            dve.wait_ge(cin, n + 1)
                            nc.vector.tensor_copy(CIN[:, :, :], pB[0:P, 0:2 * H0].rearrange("p (n h) -> p n h", h=H0))
                            dve.drain()
                        if n == 0:
                            nc.vector.tensor_tensor(F[:, :], F[:, :], B[:, :], ALU.max)
                            dve.drain()
                            nc.vector.tensor_tensor(V[:, :], V[:, :], F[:, :], ALU.subtract).then_inc(m_done, 1)
                            dve.wait_ge(ex_done, 1)
                    nc.vector.tensor_tensor(F[:, :], F[:, :], V[:, :], ALU.subtract)
                    dve.drain()
                    nc.vector.tensor_tensor(F[:, :], F[:, :], B[:, :], ALU.add)
                    dve.drain()
                    nc.vector.reciprocal(F[:, :], F[:, :])
                    dve.drain()
                    nc.vector.tensor_tensor(V[:, :], V[:, :], F[:, :], ALU.mult).then_inc(a_done, 1)
                    dve.wait_ge(rq_in, 32)
                    nc.vector.tensor_copy(BASEI[:, :], BASEF[:, :])
                    for b in range(ES // QB):
                        nc.vector.tensor_copy(OFFQ[:, b:b + 1], RQ[:, b, 0:1])
                    dve.drain()
                    for b in range(ES // QB):
                        last = nc.vector.tensor_scalar(RQ[:, b, :], RQ[:, b, :], OFFQ[:, b:b + 1], None, ALU.subtract)
                    last.then_inc(rq_done, 1)
                    for b in range(ES // QB):
                        dve.wait_ge(rt, b + 1)
                        nc.vector.tensor_copy(RELT[:, b * QB:(b + 1) * QB], pR[b % 2][0:P, 0:QB]).then_inc(rtc, 1)


def sum_segments(nc, sb, ps, sem, sems, pace, tag, TABLE, AD, iota, SRCT, RELT, BASEI, ACC):
    K = 8
    with ExitStack() as s:
        G = [[sb(s, f"G{tag}{k}_{m}", [P, D]) for m in range(K)] for k in range(2)]
        if AD is not None:
            G2 = [[sb(s, f"GW{tag}{k}_{m}", [P, D]) for m in range(K)] for k in range(2)]
            AT = [sb(s, f"AT{tag}{k}", [P, K, H0]) for k in range(2)]
        else:
            G2 = G
        HOT = [sb(s, f"HOT{tag}{k}", [P, K, P]) for k in range(2)]
        idx = [sb(s, f"idx{tag}{k}", [P, K], i32) for k in range(2)]
        pA = [ps(s, f"pA{tag}{m}", [128, 512]) for m in range(K)]
        g_in = [sem.gather(f"rows_in_{tag}{k}", K) for k in range(2)]
        g_free = sems(f"rows_free_{tag}", 2)
        a_in, a_free = sems(f"attn_in_{tag}", 2), sems(f"attn_free_{tag}", 2)
        hot, prod = sems(f"onehot_{tag}", 2), sems(f"prod_{tag}", K)
        w_ready, hot_free, pfree = sems(f"weighted_{tag}", 2), sems(f"onehot_free_{tag}", 2), sems(f"sum_bank_free_{tag}", K)
        if AD is not None:
            av = AD.rearrange("(t p) h -> p t h", p=P)
        with nc.Block() as block:
            @block.gpsimd
            def _(pool):
                with pool.Fori(0, ES // (2 * K)) as g:
                    for k in range(2):
                        hold(pool, g_free[k], g + 1, pace["pool"])
                        nc.gpsimd.tensor_copy(idx[k][:, :], SRCT[:, ds((g * 2 + k) * K, K)])
                        pool.drain()
                        for m in range(K):
                            pool.indirect_dma_start(G[k][m][:, :], None, TABLE[:, :],
                                                    bass.IndirectOffsetOnAxis(ap=idx[k][:, m:m + 1], axis=0)
                                                    ).then_inc(g_in[k][m], 16)

            if AD is not None:
                @block.sync
                def _(sp):
                    with sp.Fori(0, ES // (2 * K)) as g:
                        for k in range(2):
                            hold(sp, a_free[k], g + 1, pace["sp"])
                            sp.dma_start(AT[k][:, :, :], av[:, ds((g * 2 + k) * K, K), :]).then_inc(a_in[k], 16)

            @block.tensor
            def _(pe):
                for k in range(2):
                    pe.sem_inc(hot_free[k], 1)
                    pe.sem_inc(g_free[k], 1)
                with pe.Fori(0, ES // (2 * K)) as g:
                    for k in range(2):
                        hold(pe, hot[k], g + 1, pace["pe"])
                        for m in range(K):
                            if AD is not None:
                                hold(pe, w_ready[k], g * K + m + 1, pace["pe"])
                            else:
                                hold(pe, g_in[k][m], g * 16 + 16, pace["pe"])
                            hold(pe, pfree[m], g * 2 + k + 1, pace["pe"])
                            for c in range(KD):
                                last = nc.tensor.matmul(pA[m][:, c * P:(c + 1) * P], G2[k][m][:, c * 128:(c + 1) * 128],
                                                        HOT[k][:, m, :], start=True, stop=True)
                            last.then_inc(prod[m], 1)
                        hold(pe, prod[K - 1], g * 2 + k + 1, pace["pe"])
                        pe.sem_inc(hot_free[k], 1)
                        if AD is None:
                            pe.sem_inc(g_free[k], 1)

            @block.vector
            def _(dve):
                for k in range(2):
                    dve.sem_inc(a_free[k], 1)
                for m in range(K):
                    dve.sem_inc(pfree[m], 1)
                nc.vector.memset(ACC[:, :], 0.0)
                regs = [dve.alloc_register(f"base_{tag}{m}") for m in range(K)]
                acc = ACC[:, :].rearrange("p (c r) -> p c r", c=KD)
                with dve.Fori(0, ES // (2 * K)) as g:
                    for k in range(2):
                        t = (g * 2 + k) * K
                        hold(dve, hot_free[k], g + 1, pace["dve"])
                        nc.vector.tensor_tensor(HOT[k][:, :, :], iota[0:P, 0:P].unsqueeze(1).to_broadcast([P, K, P]),
                                                RELT[:, ds(t, K)].unsqueeze(2).to_broadcast([P, K, P]),
                                                ALU.is_equal).then_inc(hot[k], 1)
                        if AD is not None:
                            hold(dve, a_in[k], g * 16 + 16, pace["dve"])
                            for m in range(K):
                                hold(dve, g_in[k][m], g * 16 + 16, pace["dve"])
                                nc.vector.tensor_tensor(
                                    G2[k][m][:, :].rearrange("p (h d) -> p h d", d=HD),
                                    G[k][m][:, :].rearrange("p (h d) -> p h d", d=HD),
                                    AT[k][:, m, :].unsqueeze(2).to_broadcast([P, H0, HD]), ALU.mult).then_inc(w_ready[k], 1)
                            hold(dve, w_ready[k], (g + 1) * K, pace["dve"])
                            dve.sem_inc(a_free[k], 1)
                            dve.sem_inc(g_free[k], 1)
                        dve.load(regs, BASEI[0:1, ds(t, K)])
                        for m in range(K):
                            hold(dve, prod[m], g * 2 + k + 1, pace["dve"])
                            r = dve.snap(regs[m], min_val=0, max_val=N - 1)
                            nc.vector.tensor_tensor(acc[:, :, ds(r, P)], acc[:, :, ds(r, P)],
                                                    pA[m][:, 0:2 * P].rearrange("p (c r) -> p c r", c=KD),
                                                    ALU.add).then_inc(pfree[m], 1)
                            dve.drain()


def rank_rows(nc, sb, ps, sem, sems, pace, tag, ident, ACC, RSUMD):
    with ExitStack() as s:
        col = [sb(s, f"col{tag}{k}", [128, KD * P]) for k in range(2)]
        row = [sb(s, f"rrow{tag}{k}", [P, D]) for k in range(2)]
        pT = [ps(s, f"pRT{tag}{k}", [128, 512]) for k in range(2)]
        c_ready, t_ready, r_ready, r_out = (sems(f"col_ready_{tag}", 2), sems(f"rank_T_{tag}", 2),
                                            sems(f"rrow_ready_{tag}", 2), sems(f"rrow_out_{tag}", 2))
        with nc.Block() as block:
            @block.scalar
            def _(act):
                for k in range(2):
                    act.sem_inc(t_ready[k], 1)
                with act.Fori(0, NT // 2) as g:
                    for k in range(2):
                        hold(act, t_ready[k], g + 1, pace["act"])
                        v = ACC[:, :].rearrange("p (c r) -> p c r", c=KD)
                        nc.scalar.activation(col[k][:, :].rearrange("p (c r) -> p c r", c=KD),
                                             v[:, :, ds((g * 2 + k) * P, P)], ACT.Copy).then_inc(c_ready[k], 1)

            @block.tensor
            def _(pe):
                with pe.Fori(0, NT // 2) as g:
                    for k in range(2):
                        hold(pe, c_ready[k], g + 1, pace["pe"])
                        hold(pe, r_ready[k], g + 1, pace["pe"])
                        nc.tensor.transpose(pT[k][0:P, 0:128], col[k][:, 0:P], ident[:, :])
                        nc.tensor.transpose(pT[k][0:P, 128:D], col[k][:, P:2 * P], ident[:, :]).then_inc(t_ready[k], 1)

            @block.vector
            def _(dve):
                for k in range(2):
                    dve.sem_inc(r_ready[k], 1)
                with dve.Fori(0, NT // 2) as g:
                    for k in range(2):
                        hold(dve, t_ready[k], g + 2, pace["dve"])
                        hold(dve, r_out[k], g * 16 + 16, pace["dve"])
                        nc.vector.tensor_copy(row[k][:, :], pT[k][0:P, 0:D]).then_inc(r_ready[k], 1)

            @block.sync
            def _(sp):
                for k in range(2):
                    sp.sem_inc(r_out[k], 16)
                with sp.Fori(0, NT // 2) as g:
                    for k in range(2):
                        hold(sp, r_ready[k], g + 2, pace["sp"])
                        sp.dma_start(RSUMD[ds((g * 2 + k) * P, P), :], row[k][:, :]).then_inc(r_out[k], 16)
                for k in range(2):
                    sp.wait_ge(r_out[k], 16 * (NT // 2 + 1))


def add_attention(nc, sb, sem, sems, pace, RSUMD, RANKI, bias, X):
    K = 5
    b_in = sem("bias_in")
    with ExitStack() as s:
        Y = [sb(s, f"Y{k}", [P, K * D]) for k in range(2)]
        idx = [sb(s, f"yidx{k}", [P, K], i32) for k in range(2)]
        BI = sb(s, "BI", [P, D])
        y_in, y_free = sem.gather("y_in", 2), sems("y_free", 2)
        with nc.Block() as block:
            @block.sync
            def _(sp):
                sp.dma_start(BI[:, :], bias.rearrange("h d -> (h d)").partition_broadcast(P)).then_inc(b_in, 16)
                sp.wait_ge(b_in, 16)

            @block.gpsimd
            def _(pool):
                with pool.Fori(0, NT // (2 * K)) as g:
                    for k in range(2):
                        hold(pool, y_free[k], g + 1, pace["pool"])
                        nc.gpsimd.memset(Y[k][:, :], 0.0)
                        nc.gpsimd.tensor_copy(idx[k][:, :], RANKI[:, ds((g * 2 + k) * K, K)])
                        pool.drain()
                        for m in range(K):
                            pool.indirect_dma_start(Y[k][:, m * D:(m + 1) * D], None, RSUMD[:, :],
                                                    bass.IndirectOffsetOnAxis(ap=idx[k][:, m:m + 1], axis=0),
                                                    bounds_check=N - 1, oob_is_err=False).then_inc(y_in[k], 16)

            @block.vector
            def _(dve):
                for k in range(2):
                    dve.sem_inc(y_free[k], 1)
                dve.wait_ge(b_in, 16)
                with dve.Fori(0, NT // (2 * K)) as g:
                    for k in range(2):
                        hold(dve, y_in[k], g * (16 * K) + 16 * K, pace["dve"])
                        nc.vector.tensor_tensor(Y[k][:, :].rearrange("p (m d) -> p m d", d=D),
                                                Y[k][:, :].rearrange("p (m d) -> p m d", d=D),
                                                BI[:, :].unsqueeze(1).to_broadcast([P, K, D]), ALU.add)
                        dve.drain()
                        v = X[:, ds((g * 2 + k) * (K * D), K * D)]
                        nc.vector.tensor_tensor(v, v, Y[k][:, :], ALU.add)
                        dve.drain()
                        dve.sem_inc(y_free[k], 1)


def store_normed(nc, sb, sem, sems, pace, X, MEAN, RSTD, XND):
    with ExitStack() as s:
        row = [sb(s, f"nrow{k}", [P, D]) for k in range(2)]
        n_ready, n_out = sems("nrow_ready", 2), sems("nrow_out", 2)
        xv = XND.rearrange("(p i) d -> p i d", i=NT)
        with nc.Block() as block:
            @block.vector
            def _(dve):
                with dve.Fori(0, NT // 2) as g:
                    for k in range(2):
                        hold(dve, n_out[k], g * 16 + 16, pace["dve"])
                        i = g * 2 + k
                        nc.vector.tensor_scalar(row[k][:, :], X[:, ds(i * D, D)], MEAN[:, ds(i, 1)],
                                                RSTD[:, ds(i, 1)], ALU.subtract, ALU.mult).then_inc(n_ready[k], 1)

            @block.sync
            def _(sp):
                for k in range(2):
                    sp.sem_inc(n_out[k], 16)
                with sp.Fori(0, NT // 2) as g:
                    for k in range(2):
                        hold(sp, n_ready[k], g + 1, pace["sp"])
                        sp.dma_start(xv[:, ds(g * 2 + k, 1), :].rearrange("p o d -> p (o d)"),
                                     row[k][:, :]).then_inc(n_out[k], 16)
                for k in range(2):
                    sp.wait_ge(n_out[k], 16 * (NT // 2 + 1))


def gated_experts(nc, sb, ps, sem, sems, pace, sW1, sb1, sW2, sb2, sW3, sb3, eW1, eb1, eW2, eb2, eW3, eb3, gW, gb,
                  X, MEAN, RSTD, ident, ones):
    NB = NG * EH2 // 128
    with ExitStack() as s:
        w_in, w_set, w_pad = sem("ffn_w_in"), sem("ffn_w_set"), sem("ffn_w_pad")
        S1 = sb(s, "S1", [128, KD, SH1])
        S2 = sb(s, "S2", [128, KD, SH2])
        S3 = sb(s, "S3", [128, D])
        E1 = sb(s, "E1", [128, KD, NG, EH1])
        E2 = sb(s, "E2", [128, NG, 128])
        E3 = sb(s, "E3", [128, NB, D])
        EB3 = sb(s, "EB3", [NG, D])
        SB3 = sb(s, "SB3", [1, D])
        GW = sb(s, "GW", [128, KD, NG])
        GB = sb(s, "GB", [1, NG])
        B1 = sb(s, "B1s", [128, KD])
        B2 = sb(s, "B2s", [128, 1])
        C1 = sb(s, "C1", [128, NG])
        C2 = sb(s, "C2", [128, NB])
        SEL = sb(s, "SEL", [NG, NB, 128])
        xn = [sb(s, f"fxn{k}", [P, D]) for k in range(GT)]
        xT = sb(s, "fxT", [128, KD, GC])
        h1 = sb(s, "h1", [128, KD, GC])
        h2 = sb(s, "h2", [128, GC])
        e1 = sb(s, "e1", [128, NG, GC])
        e2 = sb(s, "e2", [128, NB, GC])
        e2w = sb(s, "e2w", [128, NB, GC])
        wT = sb(s, "wT", [NG, GC])
        g_ = {n: sb(s, f"gate_{n}", [P, GT, NG]) for n in ("l", "p", "eq", "m1", "q", "w")}
        r_ = {n: sb(s, f"gred_{n}", [P, GT]) for n in ("mx", "sum", "v1", "v2", "d", "e", "f", "t")}
        pT = ps(s, "fpT", [128, 512])
        pG = ps(s, "fpG", [128, 512])
        pW = ps(s, "fpW", [128, 512])
        pM = [ps(s, f"fpM{k}", [128, 512]) for k in range(3)]
        pO = [ps(s, f"fpO{k}", [128, 512]) for k in range(GT)]
        xn_ready, t_ready, x_ready = sem("fxn_ready"), sem("fxT_psum"), sem("fxT_ready")
        l_ready, w_ready, wt_ready, wt_copied, wb_ready, ex_ready, gx_ready = (
            sem("glogits"), sem("gweights"), sem("gwT"), sem("gwT_copied"), sem("gw_spread"), sem("gexp"), sem("gexp_in"))
        e2_ready, e2w_ready, o_ready, x_done = sem("e2_ready"), sem("e2w_ready"), sems("fout", GT), sem("x_updated")
        m_ready = sems("fmid", 3)
        m_read = sems("fmid_read", 3)
        NM = KD + 1 + NG + NB
        bank = [n % 3 for n in range(NM)]
        per = [bank.count(b) for b in range(3)]
        with nc.Block() as block:
            @block.sync
            def _(sp):
                loads = [
                    (S1[:, :, :], sW1.rearrange("(k p) n -> p k n", p=128)),
                    (S2[:, :, :], sW2.rearrange("(k p) n -> p k n", p=128)),
                    (S3[:, :], sW3[:, :]),
                    (EB3[:, :], eb3[:, :]), (SB3[:, :], sb3.rearrange("(o n) -> o n", o=1)),
                    (GW[:, :, :], gW.rearrange("(k p) n -> p k n", p=128)), (GB[:, :], gb.rearrange("(o n) -> o n", o=1)),
                    (B1[:, :], sb1.rearrange("(k p) -> p k", p=128)), (B2[:, :], sb2.rearrange("(p o) -> p o", o=1)),
                    (C1[:, :], eb1.rearrange("e p -> p e")),
                ]
                for k in range(KD):
                    loads.append((E1[:, k, :, :], eW1[:, k * 128:(k + 1) * 128, :].rearrange("e p n -> p e n")))
                for b in range(NB):
                    for h in range(2):
                        a = slice(h * EH2, (h + 1) * EH2)
                        loads.append((E3[a, b, :], eW3[2 * b + h, :, :]))
                        loads.append((C2[a, b:b + 1], eb2[2 * b + h, :].rearrange("(p o) -> p o", o=1)))
                sp.wait_ge(w_set, 1)
                for e in range(NG):
                    a = (e % 2) * EH2
                    loads.append((E2[:, e, a:a + EH2], eW2[e, :, :]))
                for to, of in loads:
                    sp.dma_start(to, of, allow_slow_non_contiguous=True).then_inc(w_in, 16)
                sp.wait_ge(w_in, 16 * len(loads))

            @block.gpsimd
            def _(pool):
                nc.gpsimd.memset(E2[:, :, :], 0.0).then_inc(w_set, 1)
                nc.gpsimd.memset(SEL[:, :, :], 1.0).then_inc(w_pad, 1)
                pool.wait_ge(w_pad, 1)
                nc.gpsimd.affine_select(out=SEL[:, :, :], in_=SEL[:, :, :], compare_op=ALU.is_ge, fill=0.0, base=0,
                                        pattern=[[128, NB], [1, 128]], channel_multiplier=-EH2).then_inc(w_pad, 1)
                pool.wait_ge(w_pad, 2)
                nc.gpsimd.affine_select(out=SEL[:, :, :], in_=SEL[:, :, :], compare_op=ALU.is_ge, fill=0.0, base=EH2 - 1,
                                        pattern=[[-128, NB], [-1, 128]], channel_multiplier=EH2)

        with nc.Block() as block:
            @block.vector
            def _(dve):
                with dve.Fori(0, NT // GT) as g:
                    for k in range(GT):
                        i = g * GT + k
                        nc.vector.tensor_scalar(xn[k][:, :], X[:, ds(i * D, D)], MEAN[:, ds(i, 1)],
                                                RSTD[:, ds(i, 1)], ALU.subtract, ALU.mult).then_inc(xn_ready, 1)
                    hold(dve, l_ready, g + 1, pace["dve"])
                    nc.vector.tensor_copy(g_["l"][:, :, :], pG[0:P, 0:GT * NG].rearrange("p (k e) -> p k e", e=NG))
                    dve.drain()
                    nc.vector.tensor_reduce(r_["mx"][:, :], g_["l"][:, :, :], AX.X, ALU.max)
                    dve.drain()
                    nc.vector.tensor_tensor(g_["l"][:, :, :], g_["l"][:, :, :],
                                            r_["mx"][:, :].unsqueeze(2).to_broadcast([P, GT, NG]),
                                            ALU.subtract).then_inc(gx_ready, 1)
                    hold(dve, ex_ready, g * 2 + 1, pace["dve"])
                    nc.vector.tensor_reduce(r_["sum"][:, :], g_["p"][:, :, :], AX.X, ALU.add)
                    dve.drain()
                    nc.vector.reciprocal(r_["sum"][:, :], r_["sum"][:, :])
                    dve.drain()
                    nc.vector.tensor_tensor(g_["p"][:, :, :], g_["p"][:, :, :],
                                            r_["sum"][:, :].unsqueeze(2).to_broadcast([P, GT, NG]), ALU.mult)
                    dve.drain()

                    def first_max(v, top, mark):
                        nc.vector.tensor_reduce(r_[top][:, :], v[:, :, :], AX.X, ALU.max)
                        dve.drain()
                        nc.vector.tensor_tensor(g_["eq"][:, :, :], v[:, :, :],
                                                r_[top][:, :].unsqueeze(2).to_broadcast([P, GT, NG]), ALU.is_equal)
                        nc.vector.memset(r_["t"][:, :], 1.0)
                        dve.drain()
                        for e in range(NG):
                            nc.vector.tensor_tensor(mark[:, :, e], g_["eq"][:, :, e], r_["t"][:, :], ALU.mult)
                            dve.drain()
                            nc.vector.tensor_tensor(r_["t"][:, :], r_["t"][:, :], mark[:, :, e], ALU.subtract)
                            dve.drain()

                    first_max(g_["p"], "v1", g_["m1"])
                    nc.vector.scalar_tensor_tensor(g_["q"][:, :, :], g_["m1"][:, :, :], -4.0, g_["p"][:, :, :], ALU.mult, ALU.add)
                    dve.drain()
                    first_max(g_["q"], "v2", g_["w"])
                    nc.vector.tensor_tensor(r_["d"][:, :], r_["v2"][:, :], r_["v1"][:, :], ALU.subtract).then_inc(gx_ready, 1)
                    hold(dve, ex_ready, g * 2 + 2, pace["dve"])
                    nc.vector.tensor_scalar(r_["f"][:, :], r_["e"][:, :], 1.0, None, ALU.add)
                    dve.drain()
                    nc.vector.reciprocal(r_["f"][:, :], r_["f"][:, :])
                    dve.drain()
                    nc.vector.tensor_tensor(g_["w"][:, :, :], g_["w"][:, :, :],
                                            r_["e"][:, :].unsqueeze(2).to_broadcast([P, GT, NG]), ALU.mult)
                    dve.drain()
                    nc.vector.tensor_tensor(g_["w"][:, :, :], g_["w"][:, :, :], g_["m1"][:, :, :], ALU.add)
                    dve.drain()
                    nc.vector.tensor_tensor(g_["w"][:, :, :], g_["w"][:, :, :],
                                            r_["f"][:, :].unsqueeze(2).to_broadcast([P, GT, NG]), ALU.mult).then_inc(w_ready, 1)
                    hold(dve, wt_ready, g + 1, pace["dve"])
                    nc.vector.tensor_copy(wT[:, :], pG[0:NG, 256:256 + GC]).then_inc(wt_copied, 1)
                    hold(dve, wb_ready, g + 1, pace["dve"])
                    hold(dve, e2_ready, g + 1, pace["dve"])
                    nc.vector.tensor_tensor(e2w[:, :, :], e2[:, :, :],
                                            pW[:, 0:NB * GC].rearrange("p (b c) -> p b c", c=GC), ALU.mult).then_inc(e2w_ready, 1)
                    for k in range(GT):
                        hold(dve, o_ready[k], g + 1, pace["dve"])
                        v = X[:, ds((g * GT + k) * D, D)]
                        nc.vector.tensor_tensor(v, v, pO[k][0:P, 0:D], ALU.add)
                    dve.drain()

            @block.scalar
            def _(act):
                def mid(g, n, to, b):
                    hold(act, m_ready[bank[n]], g * per[bank[n]] + n // 3 + 1, pace["act"])
                    nc.scalar.activation(to, pM[bank[n]][:, 0:GC], ACT.Relu, bias=b).then_inc(m_read[bank[n]], 1)

                with act.Fori(0, NT // GT) as g:
                    hold(act, t_ready, g + 1, pace["act"])
                    nc.scalar.activation(xT[:, :, :].rearrange("p c (k q) -> p k c q", q=P),
                                         pT[:, 0:GT * KD * P].rearrange("p (k c q) -> p k c q", c=KD, q=P),
                                         ACT.Copy).then_inc(x_ready, 1)
                    for n in range(KD):
                        mid(g, n, h1[:, n, :], B1[:, n:n + 1])
                    hold(act, gx_ready, g * 2 + 1, pace["act"])
                    nc.scalar.activation(g_["p"][:, :, :], g_["l"][:, :, :], ACT.Exp).then_inc(ex_ready, 1)
                    for e in range(NG):
                        mid(g, KD + e, e1[:, e, :], C1[:, e:e + 1])
                    mid(g, KD + NG, h2[:, :], B2[:, :])
                    for b in range(NB):
                        mid(g, KD + NG + 1 + b, e2[:, b, :], C2[:, b:b + 1])
                    act.drain()
                    act.sem_inc(e2_ready, 1)
                    hold(act, gx_ready, g * 2 + 2, pace["act"])
                    nc.scalar.activation(r_["e"][:, :], r_["d"][:, :], ACT.Exp).then_inc(ex_ready, 1)

            @block.tensor
            def _(pe):
                for b in range(3):
                    pe.sem_inc(m_read[b], 1)

                def mid(g, n, pairs):
                    hold(pe, m_read[bank[n]], g * per[bank[n]] + n // 3 + 1, pace["pe"])
                    for c, (w, v) in enumerate(pairs):
                        last = nc.tensor.matmul(pM[bank[n]][:, 0:GC], w, v, start=(c == 0), stop=(c == len(pairs) - 1))
                    last.then_inc(m_ready[bank[n]], 1)

                with pe.Fori(0, NT // GT) as g:
                    hold(pe, xn_ready, g * GT + GT, pace["pe"])
                    for k in range(GT):
                        for c in range(KD):
                            last = nc.tensor.transpose(pT[:, (k * KD + c) * P:(k * KD + c + 1) * P],
                                                       xn[k][:, c * 128:(c + 1) * 128], ident[0:P, 0:P])
                    last.then_inc(t_ready, 1)
                    hold(pe, x_ready, g + 1, pace["pe"])
                    for k in range(GT):
                        a = slice(k * P, (k + 1) * P)
                        o = pG[0:P, k * NG:(k + 1) * NG]
                        for c in range(KD):
                            nc.tensor.matmul(o, xT[:, c, a], GW[:, c, :], start=(c == 0), stop=False)
                        last = nc.tensor.matmul(o, ones[:, 0:P], GB[:, :], start=False, stop=True)
                    last.then_inc(l_ready, 1)
                    for n in range(KD):
                        mid(g, n, [(S1[:, c, n * 128:(n + 1) * 128], xT[:, c, :]) for c in range(KD)])
                    for e in range(NG):
                        mid(g, KD + e, [(E1[:, c, e, :], xT[:, c, :]) for c in range(KD)])
                    mid(g, KD + NG, [(S2[:, c, :], h1[:, c, :]) for c in range(KD)])
                    for b in range(3):
                        n = max(n for n in range(KD + NG) if bank[n] == b)
                        hold(pe, m_read[b], g * per[b] + n // 3 + 2, pace["pe"])
                    for b in range(NB):
                        mid(g, KD + NG + 1 + b, [(E2[:, 2 * b + h, :], e1[:, 2 * b + h, :]) for h in range(2)])
                    hold(pe, w_ready, g + 1, pace["pe"])
                    for k in range(GT):
                        last = nc.tensor.transpose(pG[0:NG, 256 + k * P:256 + (k + 1) * P], g_["w"][:, k, :], ident[0:P, 0:P])
                    last.then_inc(wt_ready, 1)
                    hold(pe, wt_copied, g + 1, pace["pe"])
                    for b in range(NB):
                        last = nc.tensor.matmul(pW[:, b * GC:(b + 1) * GC], SEL[:, b, :], wT[:, :], start=True, stop=True)
                    last.then_inc(wb_ready, 1)
                    hold(pe, e2w_ready, g + 1, pace["pe"])
                    for k in range(GT):
                        a = slice(k * P, (k + 1) * P)
                        o = pO[k][0:P, 0:D]
                        nc.tensor.matmul(o, h2[:, a], S3[:, :], start=True, stop=False)
                        for b in range(NB):
                            nc.tensor.matmul(o, e2w[:, b, a], E3[:, b, :], start=False, stop=False)
                        nc.tensor.matmul(o, wT[:, a], EB3[:, :], start=False, stop=False)
                        nc.tensor.matmul(o, ones[:, 0:P], SB3[:, :], start=False, stop=True).then_inc(o_ready[k], 1)


def mean_layer(nc, sb, ps, sem, sems, pace, RSUMD, RANKI, RDEG, W_src, gamma, beta, X, MEAN, RSTD, ident, epsc):
    with ExitStack() as s:
        WS = sb(s, "WS", [128, KD, D])
        GA = sb(s, "GA", [128, KD])
        BE = sb(s, "BE", [128, KD])
        Z = sb(s, "Z", [128, KD, N])
        BST = sb(s, "BST", [128, KD, NT // GT, 6])
        BMV = sb(s, "BMV", [128, KD, 2])
        SC = sb(s, "SC", [128, KD])
        SH = sb(s, "SH", [128, KD])
        Y = [sb(s, f"mY{k}", [P, GT * D]) for k in range(2)]
        idx = [sb(s, f"midx{k}", [P, GT], i32) for k in range(2)]
        ys = [sb(s, f"ys{k}", [P, D]) for k in range(GT)]
        xn = [sb(s, f"mxn{k}", [P, D]) for k in range(GT)]
        yT = sb(s, "yT", [128, KD, GC])
        zr = sb(s, "zr", [128, KD, GC])
        pT = ps(s, "mpT", [128, 512])
        pZ = ps(s, "mpZ", [128, 512])
        pO = [ps(s, f"mpO{k}", [128, 512]) for k in range(GT)]
        w_in, y_in, y_free = sem("ws_in"), sem.gather("my_in", 2), sems("my_free", 2)
        s_ready, t_ready, yT_ready, z_ready, z_read = (sem("ms_ready"), sem("mT_psum"), sem("yT_ready"), sem("z_psum"),
                                                       sem("z_read"))
        NGR = NT // GT
        with nc.Block() as block:
            @block.sync
            def _(sp):
                sp.dma_start(WS[:, :, :], W_src.rearrange("(k p) n -> p k n", p=128)).then_inc(w_in, 16)
                sp.dma_start(GA[:, :], gamma.rearrange("(k p) -> p k", p=128), allow_slow_non_contiguous=True).then_inc(w_in, 16)
                sp.dma_start(BE[:, :], beta.rearrange("(k p) -> p k", p=128), allow_slow_non_contiguous=True).then_inc(w_in, 16)
                sp.wait_ge(w_in, 48)

            @block.gpsimd
            def _(pool):
                with pool.Fori(0, NGR) as g:
                    hold(pool, y_free[0], g + 1, pace["pool"])
                    nc.gpsimd.memset(Y[0][:, :], 0.0)
                    nc.gpsimd.tensor_copy(idx[0][:, :], RANKI[:, ds(g * GT, GT)])
                    pool.drain()
                    for m in range(GT):
                        pool.indirect_dma_start(Y[0][:, m * D:(m + 1) * D], None, RSUMD[:, :],
                                                bass.IndirectOffsetOnAxis(ap=idx[0][:, m:m + 1], axis=0),
                                                bounds_check=N - 1, oob_is_err=False).then_inc(y_in[0], 16)

            @block.vector
            def _(dve):
                dve.sem_inc(y_free[0], 1)
                with dve.Fori(0, NGR) as g:
                    hold(dve, y_in[0], g * (16 * GT) + 16 * GT, pace["dve"])
                    for k in range(GT):
                        i = g * GT + k
                        nc.vector.tensor_scalar(ys[k][:, :], Y[0][:, k * D:(k + 1) * D], RDEG[:, ds(i, 1)], None, ALU.mult)
                        nc.vector.tensor_scalar(xn[k][:, :], X[:, ds(i * D, D)], MEAN[:, ds(i, 1)],
                                                RSTD[:, ds(i, 1)], ALU.subtract, ALU.mult)
                    dve.drain()
                    dve.sem_inc(y_free[0], 1)
                    dve.sem_inc(s_ready, 1)
                    hold(dve, z_ready, g + 1, pace["dve"])
                    zv = pZ[:, 0:KD * GC].rearrange("p (c q) -> p c q", q=GC)
                    nc.vector.tensor_copy(Z[:, :, ds(g * GC, GC)], zv).then_inc(z_read, 1)
                    dve.drain()
                    for c in range(KD):
                        nc.vector.bn_stats(BST[:, c, ds(g, 1), :].rearrange("p o f -> p (o f)"), Z[:, c, ds(g * GC, GC)])

            @block.scalar
            def _(act):
                with act.Fori(0, NGR) as g:
                    hold(act, t_ready, g + 1, pace["act"])
                    nc.scalar.activation(yT[:, :, :].rearrange("p c (k q) -> p k c q", q=P),
                                         pT[:, 0:GT * KD * P].rearrange("p (k c q) -> p k c q", c=KD, q=P),
                                         ACT.Copy).then_inc(yT_ready, 1)

            @block.tensor
            def _(pe):
                pe.wait_ge(w_in, 48)
                with pe.Fori(0, NGR) as g:
                    hold(pe, s_ready, g + 1, pace["pe"])
                    for k in range(GT):
                        for c in range(KD):
                            last = nc.tensor.transpose(pT[:, (k * KD + c) * P:(k * KD + c + 1) * P],
                                                       ys[k][:, c * 128:(c + 1) * 128], ident[0:P, 0:P])
                    last.then_inc(t_ready, 1)
                    hold(pe, yT_ready, g + 1, pace["pe"])
                    for m in range(KD):
                        for k in range(GT):
                            o = pZ[:, m * GC + k * P:m * GC + (k + 1) * P]
                            a = slice(m * 128, (m + 1) * 128)
                            for c in range(KD):
                                nc.tensor.matmul(o, WS[:, c, a], yT[:, c, k * P:(k + 1) * P], start=(c == 0), stop=False)
                            last = nc.tensor.matmul(o, xn[k][:, a], ident[0:P, 0:P], start=False, stop=True)
                    last.then_inc(z_ready, 1)

        agg, sq = sem("bn_agg"), sem("bn_sqrt")
        with nc.Block() as block:
            @block.vector
            def _(dve):
                for c in range(KD):
                    nc.vector.bn_aggr(BMV[:, c, :], BST[:, c, :, :].rearrange("p g f -> p (g f)"))
                dve.drain()
                nc.vector.tensor_copy(SH[:, :], BMV[:, :, 1]).then_inc(agg, 1)
                dve.wait_ge(sq, 1)
                nc.vector.reciprocal(SC[:, :], SC[:, :])
                dve.drain()
                nc.vector.tensor_tensor(SC[:, :], SC[:, :], GA[:, :], ALU.mult)
                dve.drain()
                nc.vector.tensor_tensor(SH[:, :], BMV[:, :, 0], SC[:, :], ALU.mult)
                dve.drain()
                nc.vector.tensor_tensor(SH[:, :], BE[:, :], SH[:, :], ALU.subtract)

            @block.scalar
            def _(act):
                act.wait_ge(agg, 1)
                nc.scalar.activation(SC[:, :], SH[:, :], ACT.Sqrt, bias=epsc[:, :]).then_inc(sq, 1)

        zr_ready, zt_ready, zx_done = sem("zr_ready"), sem("zT_psum"), sem("z_added")
        with nc.Block() as block:
            @block.scalar
            def _(act):
                act.sem_inc(zt_ready, 1)
                with act.Fori(0, NGR) as g:
                    hold(act, zt_ready, g + 1, pace["act"])
                    for c in range(KD):
                        last = nc.scalar.activation(zr[:, c, :], Z[:, c, ds(g * GC, GC)], ACT.Relu,
                                                    bias=SH[:, c:c + 1], scale=SC[:, c:c + 1])
                    last.then_inc(zr_ready, 1)

            @block.tensor
            def _(pe):
                pe.sem_inc(zx_done, 1)
                with pe.Fori(0, NGR) as g:
                    hold(pe, zr_ready, g + 1, pace["pe"])
                    hold(pe, zx_done, g + 1, pace["pe"])
                    for k in range(GT):
                        for c in range(KD):
                            last = nc.tensor.transpose(pO[k][0:P, c * 128:(c + 1) * 128], zr[:, c, k * P:(k + 1) * P],
                                                       ident[:, :])
                    last.then_inc(zt_ready, 1)

            @block.vector
            def _(dve):
                with dve.Fori(0, NGR) as g:
                    hold(dve, zt_ready, g + 2, pace["dve"])
                    for k in range(GT):
                        v = X[:, ds((g * GT + k) * D, D)]
                        last = nc.vector.tensor_tensor(v, v, pO[k][0:P, 0:D], ALU.add)
                    last.then_inc(zx_done, 1)


def top_experts(nc, sb, ps, sem, sems, pace, router_w, router_b, W1, b1, W2, b2, X, MEAN, RSTD, ident, iota, ones, out):
    with ExitStack() as s:
        M1 = sb(s, "M1", [128, KD, NE * EH])
        M2 = sb(s, "M2", [128, HB, D])
        RWN = sb(s, "RWN", [NE, D])
        RW = sb(s, "RW", [128, KD, NE])
        RB = sb(s, "RB", [1, NE])
        MB1 = sb(s, "MB1", [128, HB])
        MB2 = sb(s, "MB2", [NE, D])
        OFFM = sb(s, "OFFM", [NE, NE, EH], bf16)
        xn = [sb(s, f"txn{k}", [P, D]) for k in range(GT)]
        xT = sb(s, "txT", [128, KD, GC])
        LG = sb(s, "LG", [P, GT, NE])
        T8 = sb(s, "T8", [P, GT, 8])
        I8 = sb(s, "I8", [P, GT, 8], u32)
        IF = sb(s, "IF", [P, GT])
        OH = sb(s, "OH", [P, GT, NE])
        OT = sb(s, "OT", [NE, GC])
        OTB = sb(s, "OTB", [NE, GC], bf16)
        hid = sb(s, "hid", [128, HB, GC])
        O = [sb(s, f"O{k}", [P, D]) for k in range(GT)]
        pT = ps(s, "tpT", [128, 512])
        pL = ps(s, "tpL", [128, 512])
        pH = [ps(s, f"tpH{k}", [128, 512]) for k in range(4)]
        pO = [ps(s, f"tpO{k}", [128, 512]) for k in range(GT)]
        w_in, o_set, rt, rc = sem("tw_in"), sem("offm_set"), sem("router_T"), sem("router_copied")
        xn_ready, t_ready, x_ready, l_ready, oh_ready, ot_ready, ot_copied = (
            sem("txn_ready"), sem("txT_psum"), sem("txT_ready"), sem("logits"), sem("onehot_ready"), sem("onehot_T"),
            sem("onehot_Tcopied"))
        h_ready, h_read = sems("hid_psum", 4), sems("hid_read", 4)
        o_ready, O_ready, O_out = sems("tout", GT), sems("O_ready", GT), sems("O_out", GT)
        with nc.Block() as block:
            @block.sync
            def _(sp):
                n = 0
                for k in range(KD):
                    for q in range(4):
                        a = slice(q * NE // 4, (q + 1) * NE // 4)
                        sp.dma_start(M1[:, k, :].rearrange("p (e h) -> p e h", h=EH)[:, a, :],
                                     W1[a, k * 128:(k + 1) * 128, :].rearrange("e p h -> p e h")).then_inc(w_in, 16)
                        n += 16
                sp.dma_start(M2[:, :, :],
                             W2.rearrange("e h d -> (e h) d").rearrange("(b q) d -> q b d", q=128)).then_inc(w_in, 16)
                sp.dma_start(MB1[:, :], b1.rearrange("e h -> (e h)").rearrange("(b q) -> q b", q=128),
                             allow_slow_non_contiguous=True).then_inc(w_in, 16)
                sp.dma_start(RWN[:, :], router_w[:, :]).then_inc(w_in, 16)
                sp.dma_start(RB[:, :], router_b.rearrange("(o e) -> o e", o=1)).then_inc(w_in, 16)
                sp.dma_start(MB2[:, :], b2[:, :]).then_inc(w_in, 16)
                n += 80
                sp.wait_ge(w_in, n)

            @block.gpsimd
            def _(pool):
                nc.gpsimd.memset(OFFM[:, :, :], LOW).then_inc(o_set, 1)
                pool.wait_ge(o_set, 1)
                nc.gpsimd.affine_select(out=OFFM[:, :, :], in_=OFFM[:, :, :], compare_op=ALU.not_equal, fill=0.0, base=0,
                                        pattern=[[-1, NE], [0, EH]], channel_multiplier=1)

            @block.tensor
            def _(pe):
                pe.wait_ge(w_in, 16 * 13)
                for c in range(KD):
                    last = nc.tensor.transpose(pT[:, c * NE:(c + 1) * NE], RWN[:, c * 128:(c + 1) * 128], ident[0:NE, 0:NE])
                last.then_inc(rt, 1)

            @block.vector
            def _(dve):
                dve.wait_ge(rt, 1)
                nc.vector.tensor_copy(RW[:, :, :], pT[:, 0:KD * NE].rearrange("p (c e) -> p c e", e=NE))

        with nc.Block() as block:
            @block.vector
            def _(dve):
                with dve.Fori(0, NT // GT) as g:
                    for k in range(GT):
                        i = g * GT + k
                        nc.vector.tensor_scalar(xn[k][:, :], X[:, ds(i * D, D)], MEAN[:, ds(i, 1)],
                                                RSTD[:, ds(i, 1)], ALU.subtract, ALU.mult).then_inc(xn_ready, 1)
                    hold(dve, l_ready, g + 1, pace["dve"])
                    nc.vector.tensor_copy(LG[:, :, :], pL[0:P, 0:GT * NE].rearrange("p (k e) -> p k e", e=NE))
                    dve.drain()
                    for k in range(GT):
                        nc.vector.max(T8[:, k, :], LG[:, k, :])
                    dve.drain()
                    for k in range(GT):
                        nc.vector.max_index(I8[:, k, :], T8[:, k, :], LG[:, k, :])
                    dve.drain()
                    nc.vector.tensor_copy(IF[:, :], I8[:, :, 0])
                    dve.drain()
                    nc.vector.tensor_tensor(OH[:, :, :], iota[0:P, 0:NE].unsqueeze(1).to_broadcast([P, GT, NE]),
                                            IF[:, :].unsqueeze(2).to_broadcast([P, GT, NE]), ALU.is_equal).then_inc(oh_ready, 1)
                    hold(dve, ot_ready, g + 1, pace["dve"])
                    nc.vector.tensor_copy(OTB[:, :], pL[0:NE, 256:256 + GC])
                    nc.vector.tensor_copy(OT[:, :], pL[0:NE, 256:256 + GC]).then_inc(ot_copied, 1)
                    for k in range(GT):
                        hold(dve, o_ready[k], g + 1, pace["dve"])
                        hold(dve, O_out[k], g * 16 + 16, pace["dve"])
                        nc.vector.scalar_tensor_tensor(O[k][:, :], pO[k][0:P, 0:D], 0.0, X[:, ds((g * GT + k) * D, D)],
                                                       ALU.max, ALU.add).then_inc(O_ready[k], 1)

            @block.scalar
            def _(act):
                with act.Fori(0, NT // GT) as g:
                    hold(act, t_ready, g + 1, pace["act"])
                    nc.scalar.activation(xT[:, :, :].rearrange("p c (k q) -> p k c q", q=P),
                                         pT[:, 0:GT * KD * P].rearrange("p (k c q) -> p k c q", c=KD, q=P),
                                         ACT.Copy).then_inc(x_ready, 1)
                    for b in range(HB):
                        hold(act, h_ready[b % 4], g * (HB // 4) + b // 4 + 1, pace["act"])
                        nc.scalar.activation(hid[:, b, :], pH[b % 4][:, 0:GC], ACT.Relu,
                                             bias=MB1[:, b:b + 1]).then_inc(h_read[b % 4], 1)

            @block.tensor
            def _(pe):
                for b in range(4):
                    pe.sem_inc(h_read[b], 1)
                with pe.Fori(0, NT // GT) as g:
                    hold(pe, xn_ready, g * GT + GT, pace["pe"])
                    for k in range(GT):
                        for c in range(KD):
                            last = nc.tensor.transpose(pT[:, (k * KD + c) * P:(k * KD + c + 1) * P],
                                                       xn[k][:, c * 128:(c + 1) * 128], ident[0:P, 0:P])
                    last.then_inc(t_ready, 1)
                    hold(pe, x_ready, g + 1, pace["pe"])
                    for k in range(GT):
                        o = pL[0:P, k * NE:(k + 1) * NE]
                        for c in range(KD):
                            nc.tensor.matmul(o, xT[:, c, k * P:(k + 1) * P], RW[:, c, :], start=(c == 0), stop=False)
                        last = nc.tensor.matmul(o, ones[:, 0:P], RB[:, :], start=False, stop=True)
                    last.then_inc(l_ready, 1)
                    hold(pe, oh_ready, g + 1, pace["pe"])
                    for k in range(GT):
                        last = nc.tensor.transpose(pL[0:NE, 256 + k * P:256 + (k + 1) * P], OH[:, k, :], ident[0:P, 0:P])
                    last.then_inc(ot_ready, 1)
                    hold(pe, ot_copied, g + 1, pace["pe"])
                    for b in range(HB):
                        hold(pe, h_read[b % 4], g * (HB // 4) + b // 4 + 1, pace["pe"])
                        o = pH[b % 4][:, 0:GC]
                        nc.tensor.matmul(o, OFFM[:, 2 * b:2 * b + 2, :].rearrange("p e h -> p (e h)"), OTB[:, :],
                                         start=True, stop=False)
                        for c in range(KD):
                            last = nc.tensor.matmul(o, M1[:, c, b * 128:(b + 1) * 128], xT[:, c, :],
                                                    start=False, stop=(c == KD - 1))
                        last.then_inc(h_ready[b % 4], 1)
                    for b in range(4):
                        hold(pe, h_read[b], (g + 1) * (HB // 4) + 1, pace["pe"])
                    for k in range(GT):
                        a = slice(k * P, (k + 1) * P)
                        o = pO[k][0:P, 0:D]
                        nc.tensor.matmul(o, OT[:, a], MB2[:, :], start=True, stop=False)
                        for b in range(HB):
                            last = nc.tensor.matmul(o, hid[:, b, a], M2[:, b, :], start=False, stop=(b == HB - 1))
                        last.then_inc(o_ready[k], 1)

            @block.sync
            def _(sp):
                ov = out.rearrange("(p i) d -> p i d", i=NT)
                for k in range(GT):
                    sp.sem_inc(O_out[k], 16)
                with sp.Fori(0, NT // GT) as g:
                    for k in range(GT):
                        hold(sp, O_ready[k], g + 1, pace["sp"])
                        sp.dma_start(ov[:, ds(g * GT + k, 1), :].rearrange("p o d -> p (o d)"), O[k][:, :]).then_inc(O_out[k], 16)
                for k in range(GT):
                    sp.wait_ge(O_out[k], 16 * (NT // GT + 1))


_INS = ["x", "src", "dst", "edge_attr_64", "L0_gnn_W_fc", "L0_gnn_W_e", "L0_gnn_attn_h", "L0_gnn_attn_e", "L0_gnn_attn_t",
        "L0_gnn_bias", "L0_ffn_sW1", "L0_ffn_sb1", "L0_ffn_sW2", "L0_ffn_sb2", "L0_ffn_sW3", "L0_ffn_sb3", "L0_ffn_eW1",
        "L0_ffn_eb1", "L0_ffn_eW2", "L0_ffn_eb2", "L0_ffn_eW3", "L0_ffn_eb3", "L0_ffn_gW", "L0_ffn_gb", "L1_gnn_W_src",
        "L1_gnn_gamma", "L1_gnn_beta", "L1_ffn_router_w", "L1_ffn_router_b", "L1_ffn_W1", "L1_ffn_b1", "L1_ffn_W2",
        "L1_ffn_b2"]


def kernel(**inputs):
    import numpy as _np
    import concourse.bacc as _bacc
    from concourse import mybir as _mybir
    from concourse.bass_utils import run_bass_kernel_spmd as _run

    nc = _bacc.Bacc("TRN2", target_bir_lowering=False, num_devices=1)
    arrays, args = {}, []
    for name in _INS:
        a = _np.ascontiguousarray(inputs[name])
        arrays[f"in_{name}_dram"] = a
        args.append(nc.dram_tensor(f"in_{name}_dram", a.shape, _mybir.dt.from_np(a.dtype), kind="ExternalInput").ap())
    args.append(nc.dram_tensor("out_0_dram", (N, D), _mybir.dt.from_np(_np.dtype("float32")), kind="ExternalOutput").ap())
    program(nc, *args)
    r = _run(nc, [arrays], core_ids=[0])
    return r.results[0]["out_0_dram"]
```

```python
from contextlib import ExitStack, contextmanager

import concourse.bass as bass
from concourse import mybir

fp32 = mybir.dt.float32
bf16 = mybir.dt.bfloat16
i32 = mybir.dt.int32
u32 = mybir.dt.uint32
ALU = mybir.AluOpType
ACT = mybir.ActivationFunctionType
AX = mybir.AxisListType

P = 125
N, E, D = 6250, 100000, 256
NT = N // P
ES = E // P
KD = D // 128
H0, HD = 8, 32
DE = 64
NG, SH1, SH2, EH1, EH2 = 4, 256, 128, 128, 64
NE, EH = 32, 64
HB = NE * EH // 128
NR = N + P
QB = 100
EPS = 1e-5
SLOPE = 0.2
LOW = -1.0e30
SKIP = 4000000
GT = 2
GC = GT * P
ds = bass.ds


def hold(eng, sem, value, pace):
    eng.wait_ge(sem, value)
    eng.sem_inc(pace, 1)


def alternate(eng, n, first, rest):
    first(0, 0)
    with eng.Fori(0, (n - 1) // 2) as i:
        rest(i * 2, 0, True)
        rest(i * 2 + 1, 1, True)
    rest(n - 1, 0, False)


def program(nc, x, src, dst, edge_attr, W_fc, W_e, attn_h, attn_e, attn_t, bias, sW1, sb1, sW2, sb2, sW3, sb3,
            eW1, eb1, eW2, eb2, eW3, eb3, gW, gb, W_src, gamma, beta, router_w, router_b, W1, b1, W2, b2, out):
    ctx = ExitStack()

    def dram(name, shape, dt=fp32):
        return nc.dram_tensor(name, shape, dt, kind="Internal").ap()

    FT = dram("ft_rows", (N, D))
    EHD = dram("eh_rows", (N, H0))
    ETD = dram("et_rows", (N, H0))
    STARTD = dram("et_at_starts", (E, H0))
    AD = dram("attention", (E, H0))
    RANKD = dram("edge_rank", (E,))
    RSUMD = dram("sums_by_rank", (N, D))
    XND = dram("normed_rows", (N, D))

    with ctx:
        def sb(stack, name, shape, dt=fp32):
            return stack.enter_context(nc.sbuf_tensor(name, shape, dt))

        def ps(stack, name, shape, dt=fp32):
            return stack.enter_context(nc.psum_tensor(name, shape, dt))

        current = []

        def sem(name):
            current[-1][1].append(current[-1][0].enter_context(nc.semaphore(name)))
            return current[-1][1][-1]

        def gather_sem(name):
            return ctx.enter_context(nc.semaphore(name))

        @contextmanager
        def phase():
            with ExitStack() as stack:
                current.append((stack, []))
                yield
                with nc.Block() as block:
                    @block.sync
                    def _(sp):
                        for one in current[-1][1]:
                            sp.sem_clear(one)
                current.pop()

        def sems(name, n):
            return [sem(f"{name}{k}") for k in range(n)]

        sem.gather = lambda name, n=1: [gather_sem(f"{name}{k}") for k in range(n)]

        pace = {e: ctx.enter_context(nc.semaphore(f"pace_{e}")) for e in ("pe", "act", "dve", "pool", "sp")}

        X = sb(ctx, "X", [P, NT * D])
        MEAN = sb(ctx, "MEAN", [P, NT])
        RSTD = sb(ctx, "RSTD", [P, NT])
        ident = sb(ctx, "ident", [128, 128])
        iota = sb(ctx, "iota", [128, 128])
        below = sb(ctx, "below", [128, 128])
        ones = sb(ctx, "ones", [1, 128])
        epsc = sb(ctx, "epsc", [128, 1])
        DEG = sb(ctx, "DEG", [P, NT])
        RDEG = sb(ctx, "RDEG", [P, NT])
        FIRSTI = sb(ctx, "FIRSTI", [P, NT], i32)
        RANKI = sb(ctx, "RANKI", [P, NT], i32)
        SRCT = sb(ctx, "SRCT", [P, ES], i32)
        RELT = sb(ctx, "RELT", [P, ES])
        BASEI = sb(ctx, "BASEI", [1, ES], i32)

        def xt(i):
            return X[:, ds(i * D, D)]

        with phase():
            constants(nc, sem, ident, iota, below, ones, epsc)
            embed_nodes(nc, sb, ps, sem, sems, pace, x, W_fc, attn_h, attn_t, X, MEAN, RSTD, ident, epsc,
                        FT, EHD, ETD)
        with phase():
            score_edges(nc, sb, ps, sem, sems, pace, src, dst, edge_attr, W_e, attn_e, ident, iota, below,
                        EHD, ETD, STARTD, AD, RANKD, DEG, RDEG, FIRSTI, RANKI, SRCT, RELT, BASEI)
        with phase(), ExitStack() as s:
            ACC = sb(s, "ACC0", [128, KD * NR])
            sum_segments(nc, sb, ps, sem, sems, pace, "a", FT, AD, iota, SRCT, RELT, BASEI, ACC)
            rank_rows(nc, sb, ps, sem, sems, pace, "a", ident, None, ACC, RSUMD)
        with phase():
            add_attention(nc, sb, sem, sems, pace, RSUMD, RANKI, bias, X)
            norm_stats(nc, sb, sem, "b", X, MEAN, RSTD, epsc)
            gated_experts(nc, sb, ps, sem, sems, pace, sW1, sb1, sW2, sb2, sW3, sb3, eW1, eb1, eW2, eb2, eW3, eb3,
                          gW, gb, X, MEAN, RSTD, ident, ones)
        with phase(), ExitStack() as s:
            norm_stats(nc, sb, sem, "c", X, MEAN, RSTD, epsc)
            store_normed(nc, sb, sem, sems, pace, X, MEAN, RSTD, XND)
            ACC = sb(s, "ACC1", [128, KD * NR])
            sum_segments(nc, sb, ps, sem, sems, pace, "b", XND, None, iota, SRCT, RELT, BASEI, ACC)
            rank_rows(nc, sb, ps, sem, sems, pace, "b", ident, W_src, ACC, RSUMD)
        with phase():
            mean_layer(nc, sb, ps, sem, sems, pace, RSUMD, RANKI, RDEG, gamma, beta, X, MEAN, RSTD, ident, epsc)
        with phase():
            norm_stats(nc, sb, sem, "d", X, MEAN, RSTD, epsc)
            top_experts(nc, sb, ps, sem, sems, pace, router_w, router_b, W1, b1, W2, b2, X, MEAN, RSTD,
                        ident, iota, ones, out)


def constants(nc, sem, ident, iota, below, ones, epsc):
    set0 = sem("const_set")
    with nc.Block() as block:
        @block.gpsimd
        def _(pool):
            nc.gpsimd.memset(ident[:, :], 0.0).then_inc(set0, 1)
            nc.gpsimd.memset(below[:, :], 1.0).then_inc(set0, 1)
            nc.gpsimd.memset(ones[:, :], 1.0)
            nc.gpsimd.memset(epsc[:, :], EPS)
            nc.gpsimd.iota(iota[:, :], pattern=[[1, 128]], base=0, channel_multiplier=0,
                           allow_small_or_imprecise_dtypes=True)
            pool.wait_ge(set0, 2)
            nc.gpsimd.affine_select(out=ident[:, :], in_=ident[:, :], compare_op=ALU.not_equal, fill=1.0,
                                    base=0, pattern=[[-1, 128]], channel_multiplier=1)
            nc.gpsimd.affine_select(out=below[:, :], in_=below[:, :], compare_op=ALU.is_gt, fill=0.0,
                                    base=0, pattern=[[1, 128]], channel_multiplier=-1)


def norm_stats(nc, sb, sem, tag, X, MEAN, RSTD, epsc):
    stats_done, sd_done = sem(f"stats_done_{tag}"), sem(f"sd_done_{tag}")
    with ExitStack() as s:
        ST = sb(s, f"ST{tag}", [P, NT * 6])
        MV = sb(s, f"MV{tag}", [P, NT, 2])
        SD = sb(s, f"SD{tag}", [P, NT])
        with nc.Block() as block:
            @block.vector
            def _(dve):
                with dve.Fori(0, NT // 2) as g:
                    for k in range(2):
                        nc.vector.bn_stats(ST[:, ds((g * 2 + k) * 6, 6)], X[:, ds((g * 2 + k) * D, D)])
                dve.drain()
                for i in range(NT):
                    nc.vector.bn_aggr(MV[:, i, :], ST[:, i * 6:i * 6 + 6])
                dve.drain()
                nc.vector.tensor_copy(MEAN[:, :], MV[:, :, 0]).then_inc(stats_done, 1)
                dve.wait_ge(sd_done, 1)
                nc.vector.reciprocal(RSTD[:, :], SD[:, :])

            @block.scalar
            def _(act):
                act.wait_ge(stats_done, 1)
                nc.scalar.activation(SD[:, :], MV[:, :, 1], ACT.Sqrt, bias=epsc[0:P, :]).then_inc(sd_done, 1)


def embed_nodes(nc, sb, ps, sem, sems, pace, x, W_fc, attn_h, attn_t, X, MEAN, RSTD, ident, epsc, FT, EHD, ETD):
    x_in, w_in = sem("x_in"), sem("w_in")
    with ExitStack() as s:
        W = sb(s, "Wext", [128, KD, D + 2 * H0])
        AH = sb(s, "AH", [128, D])
        AT = sb(s, "ATb", [128, D])
        TMP = sb(s, "Wtmp", [128, D])
        with nc.Block() as block:
            @block.sync
            def _(sp):
                sp.dma_start(W[:, :, 0:D], W_fc.rearrange("(k p) n -> p k n", p=128)).then_inc(w_in, 16)
                sp.dma_start(AH[:, :], attn_h.rearrange("h d -> (h d)").partition_broadcast(128)).then_inc(w_in, 16)
                sp.dma_start(AT[:, :], attn_t.rearrange("h d -> (h d)").partition_broadcast(128)).then_inc(w_in, 16)
                xv = x.rearrange("(p i) d -> p (i d)", i=NT)
                sp.dma_start(X[0:112, :], xv[0:112, :], max_dma_last_dim=4096).then_inc(x_in, 16)
                sp.dma_start(X[112:P, :], xv[112:P, :], max_dma_last_dim=4096).then_inc(x_in, 16)
                sp.wait_ge(w_in, 48)
                sp.wait_ge(x_in, 32)

            @block.vector
            def _(dve):
                dve.wait_ge(w_in, 48)
                for n, a in enumerate((AH, AT)):
                    for k in range(KD):
                        nc.vector.tensor_tensor(TMP[:, :], W[:, k, 0:D], a[:, :], ALU.mult)
                        dve.drain()
                        nc.vector.tensor_reduce(W[:, k, D + n * H0:D + (n + 1) * H0],
                                                TMP[:, :].rearrange("p (h d) -> p h d", d=HD), AX.X, ALU.add)
                        dve.drain()
        norm_stats(nc, sb, sem, "a", X, MEAN, RSTD, epsc)

        WX = D + 2 * H0
        xn = [sb(s, f"xn{k}", [P, D]) for k in range(GT)]
        xnT = [sb(s, f"xnT{k}", [128, KD * P]) for k in range(GT)]
        row = [sb(s, f"row{k}", [P, WX]) for k in range(GT)]
        pT = [ps(s, f"pT{k}", [128, 512]) for k in range(GT)]
        pF = [ps(s, f"pF{k}", [128, 512]) for k in range(GT)]
        xn_ready, xn_free = sems("xn_ready", GT), sems("xn_free", GT)
        t_ready, xT_ready, xT_free = sems("t_ready", GT), sems("xT_ready", GT), sems("xT_free", GT)
        f_ready, row_ready, row_free = sems("f_ready", GT), sems("row_ready", GT), sems("row_free", GT)
        stored = sems("row_stored", GT)
        ftv = FT.rearrange("(p i) d -> p i d", i=NT)
        ehv = EHD.rearrange("(p i) d -> p i d", i=NT)
        etv = ETD.rearrange("(p i) d -> p i d", i=NT)
        with nc.Block() as block:
            @block.vector
            def _(dve):
                with dve.Fori(0, NT // GT) as g:
                    for k in range(GT):
                        hold(dve, xn_free[k], g + 1, pace["dve"])
                        i = g * GT + k
                        nc.vector.tensor_scalar(xn[k][:, :], X[:, ds(i * D, D)], MEAN[:, ds(i, 1)],
                                                RSTD[:, ds(i, 1)], ALU.subtract, ALU.mult).then_inc(xn_ready[k], 1)

            @block.tensor
            def _(pe):
                for k in range(GT):
                    pe.sem_inc(xn_free[k], 1)
                    pe.sem_inc(xT_free[k], 1)
                with pe.Fori(0, NT // GT) as g:
                    for k in range(GT):
                        hold(pe, xn_ready[k], g + 1, pace["pe"])
                        nc.tensor.transpose(pT[k][:, 0:P], xn[k][:, 0:128], ident[0:P, 0:P])
                        nc.tensor.transpose(pT[k][:, P:2 * P], xn[k][:, 128:D], ident[0:P, 0:P]).then_inc(t_ready[k], 1)
                        pe.sem_inc(pace["pe"], 1)
                    for k in range(GT):
                        hold(pe, xT_ready[k], g + 1, pace["pe"])
                        pe.sem_inc(xn_free[k], 1)
                        hold(pe, row_free[k], g + 1, pace["pe"])
                        for c in range(KD):
                            last = nc.tensor.matmul(pF[k][0:P, 0:WX], xnT[k][:, c * P:(c + 1) * P], W[:, c, :],
                                                    start=(c == 0), stop=(c == KD - 1))
                        last.then_inc(f_ready[k], 1)

            @block.scalar
            def _(act):
                for k in range(GT):
                    act.sem_inc(row_free[k], 1)
                with act.Fori(0, NT // GT) as g:
                    for k in range(GT):
                        hold(act, t_ready[k], g + 1, pace["act"])
                        nc.scalar.activation(xnT[k][:, :], pT[k][:, 0:2 * P], ACT.Copy).then_inc(xT_ready[k], 1)
                    for k in range(GT):
                        hold(act, f_ready[k], g + 1, pace["act"])
                        hold(act, stored[k], g * 48 + 48, pace["act"])
                        nc.scalar.activation(row[k][:, :], pF[k][0:P, 0:WX], ACT.Copy).then_inc(row_ready[k], 1)
                        hold(act, row_ready[k], g + 1, pace["act"])
                        act.sem_inc(row_free[k], 1)

            @block.sync
            def _(sp):
                for k in range(GT):
                    sp.sem_inc(stored[k], 48)
                with sp.Fori(0, NT // GT) as g:
                    for k in range(GT):
                        hold(sp, row_ready[k], g + 1, pace["sp"])
                        i = g * GT + k
                        for to, a, b in ((ftv, 0, D), (ehv, D, D + H0), (etv, D + H0, WX)):
                            sp.dma_start(to[:, ds(i, 1), :].rearrange("p o d -> p (o d)"),
                                         row[k][:, a:b]).then_inc(stored[k], 16)
                for k in range(GT):
                    sp.wait_ge(stored[k], 48 * (NT // GT + 1))


def score_edges(nc, sb, ps, sem, sems, pace, src, dst, edge_attr, W_e, attn_e, ident, iota, below,
                EHD, ETD, STARTD, AD, RANKD, DEG, RDEG, FIRSTI, RANKI, SRCT, RELT, BASEI):
    C = 16
    NCH = ES // C
    with ExitStack() as s:
        V = sb(s, "V", [P, ES * H0])
        F = sb(s, "F", [P, ES * H0])
        DX = sb(s, "DX", [P, ES + 2])
        DXI = sb(s, "DXI", [P, ES + 2], i32)
        SRCS = sb(s, "SRCS", [P, ES], i32)
        ZB = sb(s, "ZB", [128, 128], bf16)
        with ExitStack() as t:
            QI = sb(t, "QI", [QB, ES // QB, P], i32)
            QF = sb(t, "QF", [QB, ES // QB, P])
            ebuf = [sb(t, f"ebuf{k}", [P, C * DE]) for k in range(2)]
            eT = [sb(t, f"eT{k}", [128, C // 2 * P]) for k in range(2)]
            ehs = [sb(t, f"ehs{k}", [P, C * H0]) for k in range(2)]
            idx = [sb(t, f"idx{k}", [P, C], i32) for k in range(2)]
            hotA = [sb(t, f"hotA{k}", [P, C, P], bf16) for k in range(2)]
            hotB = [sb(t, f"hotB{k}", [P, C, NT], bf16) for k in range(2)]
            DA = sb(t, "DA", [P, ES])
            DB = sb(t, "DB", [P, ES])
            WE = sb(t, "WE", [128, D])
            AE = sb(t, "AE", [128, D])
            VB = sb(t, "VB", [128, 2 * H0])
            pQ = ps(t, "pQ", [128, 512])
            pE = [ps(t, f"pE{k}", [128, 512]) for k in range(2)]
            pX = [ps(t, f"pX{k}", [128, 512]) for k in range(2)]
            pS = [ps(t, f"pS{k}", [128, 512]) for k in range(2)]
            pH = ps(t, "pH", [128, 512])

            ld, wld, prep, qt, qc = sem("idx_in"), sem("we_in"), sem("idx_prep"), sem("q_transposed"), sem("q_copied")
            zero_in = sem("starts_zeroed")
            with nc.Block() as block:
                @block.sync
                def _(sp):
                    sv, dv = (a.rearrange("(p j) -> p j", j=ES) for a in (src, dst))
                    sp.dma_start(SRCS[:, :], sv).then_inc(ld, 16)
                    sp.dma_start(DXI[:, 1:ES + 1], dv).then_inc(ld, 16)
                    sp.dma_start(QI[:, :, :], src.rearrange("(b q p) -> q b p", q=QB, p=P)).then_inc(ld, 16)
                    sp.wait_ge(prep, 1)
                    sp.dma_start(DXI[1:P, 0:1], dv[0:P - 1, ES - 1:ES], allow_slow_non_contiguous=True).then_inc(ld, 16)
                    sp.dma_start(DXI[0:P - 1, ES + 1:ES + 2], dv[1:P, 0:1], allow_slow_non_contiguous=True).then_inc(ld, 16)
                    for k in range(2):
                        sp.dma_start(WE[k * DE:(k + 1) * DE, :], W_e[:, :]).then_inc(wld, 16)
                    sp.dma_start(AE[:, :], attn_e.rearrange("h d -> (h d)").partition_broadcast(128)).then_inc(wld, 16)
                    sp.dma_start(STARTD.rearrange("(p j) h -> p (j h)", j=ES), F[:, :]).then_inc(zero_in, 16)
                    sp.wait_ge(zero_in, 16)

                @block.vector
                def _(dve):
                    nc.vector.memset(DXI[:, 0:1], -1)
                    nc.vector.memset(DXI[:, ES + 1:ES + 2], -2)
                    nc.vector.memset(F[:, :], 0.0).then_inc(prep, 1)
                    nc.vector.memset(VB[:, :], 0.0)
                    nc.vector.memset(ZB[:, :], 0.0)
                    dve.wait_ge(ld, 80)
                    nc.vector.tensor_copy(QF[:, :, :], QI[:, :, :]).then_inc(prep, 1)
                    nc.vector.tensor_copy(DX[:, :], DXI[:, :])
                    dve.drain()
                    nc.vector.tensor_scalar(DB[:, :], DX[:, 1:ES + 1], (NT - 1) / 2.0, 1.0 / NT, ALU.subtract, ALU.mult)
                    dve.drain()
                    nc.vector.tensor_scalar(DB[:, :], DB[:, :], 12582912.0, None, ALU.add)
                    dve.drain()
                    nc.vector.tensor_scalar(DA[:, :], DB[:, :], 12582912.0, None, ALU.subtract)
                    dve.drain()
                    nc.vector.scalar_tensor_tensor(DB[:, :], DA[:, :], -float(NT), DX[:, 1:ES + 1], ALU.mult, ALU.add)
                    dve.wait_ge(wld, 48)
                    nc.vector.tensor_tensor(WE[:, :], WE[:, :], AE[:, :], ALU.mult)
                    dve.drain()
                    for k in range(2):
                        a = slice(k * DE, (k + 1) * DE)
                        nc.vector.tensor_reduce(VB[a, k * H0:(k + 1) * H0],
                                                WE[a, :].rearrange("p (h d) -> p h d", d=HD), AX.X, ALU.add)
                    for b in range(ES // QB):
                        dve.wait_ge(qt, b + 1)
                        nc.vector.tensor_copy(SRCT[:, b * QB:(b + 1) * QB], pQ[0:P, 0:QB]).then_inc(qc, 1)

                @block.tensor
                def _(pe):
                    pe.wait_ge(prep, 2)
                    for b in range(ES // QB):
                        if b:
                            pe.wait_ge(qc, b)
                        nc.tensor.transpose(pQ[0:P, 0:QB], QF[:, b, :], ident[0:QB, 0:QB]).then_inc(qt, 1)

            e_in, e_free = sems("attr_in", 2), sems("attr_free", 2)
            g_in, g_free = sem.gather("eh_in", 2), sems("eh_free", 2)
            idx_ready = sems("idx_ready", 2)
            tr, cp = sems("attr_T", 2), sems("attr_Tcopied", 2)
            sc, sc_free = sems("edge_scores", 2), sems("edge_scores_free", 2)
            hot, hot_free = sems("hot", 2), sems("hot_free", 2)
            ev = edge_attr.rearrange("(p j) d -> p (j d)", j=ES)
            with nc.Block() as block:
                @block.gpsimd
                def _(pool):
                    with pool.Fori(0, NCH // 2) as g:
                        for k in range(2):
                            hold(pool, g_free[k], g + 1, pace["pool"])
                            nc.gpsimd.tensor_copy(idx[k][:, :], SRCS[:, ds((g * 2 + k) * C, C)]).then_inc(idx_ready[k], 1)
                            hold(pool, idx_ready[k], g + 1, pace["pool"])
                            for m in range(C):
                                pool.indirect_dma_start(ehs[k][:, m * H0:(m + 1) * H0], None, EHD[:, :],
                                                        bass.IndirectOffsetOnAxis(ap=idx[k][:, m:m + 1], axis=0)
                                                        ).then_inc(g_in[k], 16)

                @block.sync
                def _(sp):
                    with sp.Fori(0, NCH // 2) as g:
                        for k in range(2):
                            hold(sp, e_free[k], g + 1, pace["sp"])
                            j = (g * 2 + k) * (C * DE)
                            sp.dma_start(ebuf[k][:, :], ev[:, ds(j, C * DE)]).then_inc(e_in[k], 16)

                @block.tensor
                def _(pe):
                    for k in range(2):
                        pe.sem_inc(e_free[k], 1)
                        pe.sem_inc(hot_free[k], 1)
                    nc.tensor.matmul(pH[0:P, 0:NT], ZB[0:P, 0:P], ZB[0:P, 0:NT], start=True, stop=False,
                                     skip_group_check=True)
                    with pe.Fori(0, NCH // 2) as g:
                        for k in range(2):
                            hold(pe, e_in[k], g * 16 + 16, pace["pe"])
                            for m in range(C // 2):
                                to = (pE, pX)[m // 4][k]
                                last = nc.tensor.transpose(to[:, (m % 4) * P:(m % 4 + 1) * P],
                                                           ebuf[k][:, m * 2 * DE:(m + 1) * 2 * DE], ident[0:P, 0:P])
                            last.then_inc(tr[k], 1)
                            hold(pe, hot[k], g + 1, pace["pe"])
                            for m in range(C):
                                last = nc.tensor.matmul(pH[0:P, 0:NT], hotA[k][:, m, :], hotB[k][:, m, :],
                                                        start=False, stop=False, skip_group_check=True)
                            last.then_inc(hot_free[k], 1)
                            hold(pe, cp[k], g + 1, pace["pe"])
                            pe.sem_inc(e_free[k], 1)
                            hold(pe, sc_free[k], g + 1, pace["pe"])
                            for m in range(C // 2):
                                last = nc.tensor.matmul(pS[k][0:P, m * 2 * H0:(m + 1) * 2 * H0],
                                                        eT[k][:, m * P:(m + 1) * P], VB[:, :], start=True, stop=True)
                            last.then_inc(sc[k], 1)
                    nc.tensor.matmul(pH[0:P, 0:NT], ZB[0:P, 0:P], ZB[0:P, 0:NT], start=False, stop=True,
                                     skip_group_check=True)

                @block.scalar
                def _(act):
                    with act.Fori(0, NCH // 2) as g:
                        for k in range(2):
                            hold(act, tr[k], g + 1, pace["act"])
                            hold(act, sc_free[k], g + 1, pace["act"])
                            nc.scalar.activation(eT[k][:, 0:4 * P], pE[k][:, 0:4 * P], ACT.Copy)
                            nc.scalar.activation(eT[k][:, 4 * P:8 * P], pX[k][:, 0:4 * P], ACT.Copy).then_inc(cp[k], 1)

                @block.vector
                def _(dve):
                    for k in range(2):
                        dve.sem_inc(g_free[k], 1)
                        dve.sem_inc(sc_free[k], 1)
                    with dve.Fori(0, NCH // 2) as g:
                        for k in range(2):
                            j = (g * 2 + k) * C
                            hold(dve, hot_free[k], g + 1, pace["dve"])
                            for to, a, w in ((hotA, DA, P), (hotB, DB, NT)):
                                last = nc.vector.tensor_tensor(
                                    to[k][:, :, :], iota[0:P, 0:w].unsqueeze(1).to_broadcast([P, C, w]),
                                    a[:, ds(j, C)].unsqueeze(2).to_broadcast([P, C, w]), ALU.is_equal)
                            last.then_inc(hot[k], 1)
                            hold(dve, sc[k], g + 1, pace["dve"])
                            hold(dve, g_in[k], g * (16 * C) + 16 * C, pace["dve"])
                            nc.vector.tensor_tensor(V[:, ds(j * H0, C * H0)], pS[k][0:P, 0:C * H0], ehs[k][:, :],
                                                    ALU.add).then_inc(sc_free[k], 1)
                            hold(dve, sc_free[k], g + 2, pace["dve"])
                            dve.sem_inc(g_free[k], 1)

            tot, pre = sem("node_totals"), sem("node_prefix")
            INC = sb(t, "INC", [P, 2, NT])
            NEQ = sb(t, "NEQ", [P, NT])
            UN = sb(t, "UN", [P, NT])
            TOT = sb(t, "TOT", [P, 2])
            with nc.Block() as block:
                @block.vector
                def _(dve):
                    nc.vector.tensor_copy(DEG[:, :], pH[0:P, 0:NT])
                    nc.vector.memset(UN[:, :], 1.0)
                    dve.drain()
                    nc.vector.tensor_scalar(NEQ[:, :], DEG[:, :], 1.0, None, ALU.min)
                    nc.vector.tensor_scalar(RDEG[:, :], DEG[:, :], 1.0, None, ALU.max)
                    dve.drain()
                    nc.vector.reciprocal(RDEG[:, :], RDEG[:, :])
                    nc.vector.tensor_tensor_scan(INC[:, 0, :], UN[:, :], DEG[:, :], 0.0, ALU.mult, ALU.add)
                    nc.vector.tensor_tensor_scan(INC[:, 1, :], UN[:, :], NEQ[:, :], 0.0, ALU.mult, ALU.add)
                    dve.drain()
                    nc.vector.tensor_copy(TOT[:, :], INC[:, :, NT - 1]).then_inc(tot, 1)
                    dve.drain()
                    nc.vector.tensor_tensor(INC[:, 0, :], INC[:, 0, :], DEG[:, :], ALU.subtract)
                    nc.vector.tensor_tensor(INC[:, 1, :], INC[:, 1, :], NEQ[:, :], ALU.subtract)
                    nc.vector.tensor_scalar(UN[:, :], NEQ[:, :], 1.0, -float(SKIP), ALU.subtract, ALU.mult)
                    dve.drain()
                    dve.wait_ge(pre, 1)
                    for n, to in enumerate((FIRSTI, RANKI)):
                        nc.vector.scalar_tensor_tensor(to[:, :], INC[:, n, :], pQ[0:P, n:n + 1], UN[:, :], ALU.add, ALU.add)

                @block.tensor
                def _(pe):
                    pe.wait_ge(tot, 1)
                    for n in range(2):
                        last = nc.tensor.matmul(pQ[0:P, n:n + 1], below[0:P, 0:P], TOT[:, n:n + 1], start=True, stop=True)
                    last.then_inc(pre, 1)


        st_et = sem.gather("et_loaded")[0]
        with ExitStack() as t:
            ETS = sb(t, "ETS", [P, NT * H0])
            K = 10
            islot = [sb(t, f"islot{k}", [P, K], i32) for k in range(2)]
            eslot = [sb(t, f"eslot{k}", [P, K * H0]) for k in range(2)]
            st = sem.gather("starts", 2)
            with nc.Block() as block:
                @block.gpsimd
                def _(pool):
                    pool.dma_start(ETS[:, :], ETD.rearrange("(p i) h -> p (i h)", i=NT)).then_inc(st_et, 16)
                    pool.wait_ge(st_et, 16)
                    for n in range(NT // K):
                        k = n % 2
                        if n >= 2:
                            pool.wait_ge(st[k], 16 * K * (n // 2))
                        nc.gpsimd.tensor_copy(islot[k][:, :], FIRSTI[:, n * K:(n + 1) * K])
                        nc.gpsimd.tensor_copy(eslot[k][:, :], ETS[:, n * K * H0:(n + 1) * K * H0])
                        pool.drain()
                        for m in range(K):
                            pool.indirect_dma_start(STARTD[:, :], bass.IndirectOffsetOnAxis(ap=islot[k][:, m:m + 1], axis=0),
                                                    eslot[k][:, m * H0:(m + 1) * H0], None,
                                                    bounds_check=E - 1, oob_is_err=False).then_inc(st[k], 16)
                    for k in range(2):
                        pool.wait_ge(st[k], 16 * K * ((NT // K + 1 - k) // 2))

        with ExitStack() as t:
            B = sb(t, "B", [P, ES * H0])
            CONT = sb(t, "CONT", [P, ES + 1])
            PEN = sb(t, "PEN", [P, ES + 1])
            RK = sb(t, "RK", [P, ES])
            ONE = sb(t, "ONE", [P, ES])
            C0 = sb(t, "C0", [P, H0])
            ALLC = sb(t, "ALLC", [P, 2, H0])
            ENDS = sb(t, "ENDS", [P, 2, H0])
            CH = sb(t, "CH", [H0, 4 * P])
            CP = sb(t, "CP", [H0, 2 * P])
            CARRY = sb(t, "CARRY", [H0, 2, P + 1])
            CIN = sb(t, "CIN", [P, 2, H0])
            OFF = sb(t, "OFF", [P, 1])
            TOTR = sb(t, "TOTR", [P, 1])
            RQ = sb(t, "RQ", [QB, ES // QB, P])
            OFFQ = sb(t, "OFFQ", [QB, ES // QB])
            BASEF = sb(t, "BASEF", [1, ES])
            pC = ps(t, "pC", [128, 512])
            pB = ps(t, "pB", [128, 512])
            pR = [ps(t, f"pR{k}", [128, 512]) for k in range(2)]
            in_, c0_in, m_done, ex_done = sem("starts_in"), sem.gather("c0_in")[0], sem("max_done"), sem("exp_done")
            ends, chain, carr, cin = sem("ends"), sem("chain"), sem("carries"), sem("carries_in")
            rtot, rpre, rk_done = sem("rank_totals"), sem("rank_prefix"), sem("ranks_done")
            rk_out, rq_in, rq_done, rt, rtc = (sem("ranks_out"), sem("ranks_in"), sem("ranks_rel"), sem("ranks_T"),
                                               sem("ranks_Tcopied"))
            a_done, a_out = sem("attn_done"), sem("attn_out")

            def head(buf, h, back=False):
                v = buf[:, :].rearrange("p (j h) -> p j h", h=H0)[:, :, h]
                return v[:, ::-1] if back else v

            with nc.Block() as block:
                @block.gpsimd
                def _(pool):
                    pool.indirect_dma_start(C0[:, :], None, ETD[:, :],
                                            bass.IndirectOffsetOnAxis(ap=DXI[:, 1:2], axis=0)).then_inc(c0_in, 16)

                @block.sync
                def _(sp):
                    sp.dma_start(F[:, :], STARTD.rearrange("(p j) h -> p (j h)", j=ES)).then_inc(in_, 16)
                    sp.wait_ge(rk_done, 1)
                    sp.dma_start(RANKD.rearrange("(p j) -> p j", j=ES), RK[:, :]).then_inc(rk_out, 16)
                    sp.wait_ge(rk_out, 16)
                    sp.dma_start(RQ[:, :, :], RANKD.rearrange("(b q p) -> q b p", q=QB, p=P)).then_inc(rq_in, 16)
                    sp.dma_start(BASEF[:, :], RANKD.rearrange("(o t p) -> o t p", o=1, p=P)[:, :, 0],
                                 allow_slow_non_contiguous=True).then_inc(rq_in, 16)
                    sp.wait_ge(a_done, 1)
                    sp.dma_start(AD.rearrange("(p j) h -> p (j h)", j=ES), V[:, :]).then_inc(a_out, 16)
                    sp.wait_ge(a_out, 16)

                @block.scalar
                def _(act):
                    act.wait_ge(m_done, 1)
                    nc.scalar.activation(V[:, :], V[:, :], ACT.Exp).then_inc(ex_done, 1)

                @block.tensor
                def _(pe):
                    pe.wait_ge(rtot, 1)
                    nc.tensor.matmul(pR[0][0:P, 0:1], below[0:P, 0:P], TOTR[:, :], start=True, stop=True).then_inc(rpre, 1)
                    for n in range(2):
                        pe.wait_ge(ends, n + 1)
                        for c, v in enumerate((ENDS[:, 0, :], ENDS[:, 1, :], ALLC[:, 0, :], ALLC[:, 1, :])):
                            last = nc.tensor.transpose(pC[0:H0, c * P:(c + 1) * P], v, ident[0:P, 0:P])
                        last.then_inc(chain, 1)
                        pe.wait_ge(carr, n + 1)
                        nc.tensor.transpose(pB[0:P, 0:H0], CARRY[:, 0, 0:P], ident[0:H0, 0:H0])
                        nc.tensor.transpose(pB[0:P, H0:2 * H0], CARRY[:, 1, 1:P + 1], ident[0:H0, 0:H0]).then_inc(cin, 1)
                    for b in range(ES // QB):
                        pe.wait_ge(rq_done, 1)
                        if b >= 2:
                            pe.wait_ge(rtc, b - 1)
                        nc.tensor.transpose(pR[b % 2][0:P, 0:QB], RQ[:, b, :], ident[0:QB, 0:QB]).then_inc(rt, 1)

                @block.vector
                def _(dve):
                    nc.vector.tensor_tensor(CONT[:, :], DX[:, 1:ES + 2], DX[:, 0:ES + 1], ALU.is_equal)
                    nc.vector.memset(ONE[:, :], 1.0)
                    dve.drain()
                    nc.vector.tensor_scalar(PEN[:, :], CONT[:, :], 1.0, -LOW, ALU.subtract, ALU.mult)
                    nc.vector.tensor_scalar(RK[:, :], CONT[:, 0:ES], -1.0, 1.0, ALU.mult, ALU.add)
                    for n in range(2):
                        nc.vector.tensor_reduce(OFF[:, :], CONT[:, n:n + ES], AX.X, ALU.min)
                        dve.drain()
                        nc.vector.tensor_copy(ALLC[:, n, :], OFF[:, 0:1].to_broadcast([P, H0]))
                        dve.drain()
                    nc.vector.tensor_tensor_scan(RK[:, :], ONE[:, :], RK[:, :], 0.0, ALU.mult, ALU.add)
                    dve.drain()
                    nc.vector.tensor_copy(TOTR[:, :], RK[:, ES - 1:ES]).then_inc(rtot, 1)
                    dve.wait_ge(rpre, 1)
                    nc.vector.tensor_scalar(OFF[:, :], pR[0][0:P, 0:1], 1.0, None, ALU.subtract)
                    dve.drain()
                    nc.vector.tensor_scalar(RK[:, :], RK[:, :], OFF[:, :], None, ALU.add).then_inc(rk_done, 1)
                    dve.wait_ge(in_, 16)
                    dve.wait_ge(c0_in, 16)
                    for h in range(H0):
                        nc.vector.tensor_tensor_scan(head(F, h), CONT[:, 0:ES], head(F, h), C0[:, h:h + 1], ALU.mult, ALU.add)
                    dve.drain()
                    nc.vector.tensor_tensor(V[:, :], V[:, :], F[:, :], ALU.add)
                    dve.drain()
                    nc.vector.scalar_tensor_tensor(V[:, :], V[:, :], SLOPE, V[:, :], ALU.mult, ALU.max)
                    dve.drain()
                    for n, (data, first, op0, op1) in enumerate(((PEN, LOW, ALU.add, ALU.max),
                                                                 (CONT, 0.0, ALU.mult, ALU.add))):
                        for r in range(2):
                            for h in range(H0):
                                f0 = first if r == 0 else CIN[:, 0, h:h + 1]
                                b0 = first if r == 0 else CIN[:, 1, h:h + 1]
                                nc.vector.tensor_tensor_scan(head(F, h), data[:, 0:ES], head(V, h), f0, op0, op1)
                                nc.vector.tensor_tensor_scan(head(B, h, True), data[:, 1:ES + 1][:, ::-1],
                                                             head(V, h, True), b0, op0, op1)
                            dve.drain()
                            if r:
                                continue
                            nc.vector.tensor_copy(ENDS[:, 0, :], F[:, (ES - 1) * H0:ES * H0])
                            nc.vector.tensor_copy(ENDS[:, 1, :], B[:, 0:H0]).then_inc(ends, 1)
                            dve.wait_ge(chain, n + 1)
                            nc.vector.tensor_copy(CH[:, :], pC[0:H0, 0:4 * P])
                            dve.drain()
                            if n == 0:
                                nc.vector.tensor_scalar(CP[:, :], CH[:, 2 * P:4 * P], 1.0, -LOW, ALU.subtract, ALU.mult)
                            else:
                                nc.vector.tensor_copy(CP[:, :], CH[:, 2 * P:4 * P])
                            nc.vector.memset(CARRY[:, 0, 0:1], first)
                            nc.vector.memset(CARRY[:, 1, P:P + 1], first)
                            dve.drain()
                            nc.vector.tensor_tensor_scan(CARRY[:, 0, 1:P + 1], CP[:, 0:P], CH[:, 0:P], first, op0, op1)
                            nc.vector.tensor_tensor_scan(CARRY[:, 1, 0:P][:, ::-1], CP[:, P:2 * P][:, ::-1],
                                                         CH[:, P:2 * P][:, ::-1], first, op0, op1).then_inc(carr, 1)
                            dve.wait_ge(cin, n + 1)
                            nc.vector.tensor_copy(CIN[:, :, :], pB[0:P, 0:2 * H0].rearrange("p (n h) -> p n h", h=H0))
                            dve.drain()
                        if n == 0:
                            nc.vector.tensor_tensor(F[:, :], F[:, :], B[:, :], ALU.max)
                            dve.drain()
                            nc.vector.tensor_tensor(V[:, :], V[:, :], F[:, :], ALU.subtract).then_inc(m_done, 1)
                            dve.wait_ge(ex_done, 1)
                    nc.vector.tensor_tensor(F[:, :], F[:, :], V[:, :], ALU.subtract)
                    dve.drain()
                    nc.vector.tensor_tensor(F[:, :], F[:, :], B[:, :], ALU.add)
                    dve.drain()
                    nc.vector.reciprocal(F[:, :], F[:, :])
                    dve.drain()
                    nc.vector.tensor_tensor(V[:, :], V[:, :], F[:, :], ALU.mult).then_inc(a_done, 1)
                    dve.wait_ge(rq_in, 32)
                    nc.vector.tensor_copy(BASEI[:, :], BASEF[:, :])
                    for b in range(ES // QB):
                        nc.vector.tensor_copy(OFFQ[:, b:b + 1], RQ[:, b, 0:1])
                    dve.drain()
                    for b in range(ES // QB):
                        last = nc.vector.tensor_scalar(RQ[:, b, :], RQ[:, b, :], OFFQ[:, b:b + 1], None, ALU.subtract)
                    last.then_inc(rq_done, 1)
                    for b in range(ES // QB):
                        dve.wait_ge(rt, b + 1)
                        nc.vector.tensor_copy(RELT[:, b * QB:(b + 1) * QB], pR[b % 2][0:P, 0:QB]).then_inc(rtc, 1)


def sum_segments(nc, sb, ps, sem, sems, pace, tag, TABLE, AD, iota, SRCT, RELT, BASEI, ACC):
    K = 8
    with ExitStack() as s:
        G = [[sb(s, f"G{tag}{k}_{m}", [P, D]) for m in range(K)] for k in range(2)]
        if AD is not None:
            G2 = [[sb(s, f"GW{tag}{k}_{m}", [P, D]) for m in range(K)] for k in range(2)]
            AT = [sb(s, f"AT{tag}{k}", [P, K, H0]) for k in range(2)]
        else:
            G2 = G
        HOT = [sb(s, f"HOT{tag}{k}", [P, K, P]) for k in range(2)]
        idx = [sb(s, f"idx{tag}{k}", [P, K], i32) for k in range(2)]
        pA = [ps(s, f"pA{tag}{m}", [128, 512]) for m in range(K)]
        g_in = [sem.gather(f"rows_in_{tag}{k}", K) for k in range(2)]
        g_free, idx_ready = sems(f"rows_free_{tag}", 2), sems(f"idx_ready_{tag}", 2)
        a_in, a_free = sems(f"attn_in_{tag}", 2), sems(f"attn_free_{tag}", 2)
        hot, prod = sems(f"onehot_{tag}", 2), sems(f"prod_{tag}", K)
        w_ready, hot_free, pfree = sems(f"weighted_{tag}", 2), sems(f"onehot_free_{tag}", 2), sems(f"sum_bank_free_{tag}", K)
        if AD is not None:
            av = AD.rearrange("(t p) h -> p t h", p=P)
        with nc.Block() as block:
            @block.gpsimd
            def _(pool):
                with pool.Fori(0, ES // (2 * K)) as g:
                    for k in range(2):
                        hold(pool, g_free[k], g + 1, pace["pool"])
                        nc.gpsimd.tensor_copy(idx[k][:, :], SRCT[:, ds((g * 2 + k) * K, K)]).then_inc(idx_ready[k], 1)
                        hold(pool, idx_ready[k], g + 1, pace["pool"])
                        for m in range(K):
                            pool.indirect_dma_start(G[k][m][:, :], None, TABLE[:, :],
                                                    bass.IndirectOffsetOnAxis(ap=idx[k][:, m:m + 1], axis=0)
                                                    ).then_inc(g_in[k][m], 16)

            if AD is not None:
                @block.sync
                def _(sp):
                    with sp.Fori(0, ES // (2 * K)) as g:
                        for k in range(2):
                            hold(sp, a_free[k], g + 1, pace["sp"])
                            sp.dma_start(AT[k][:, :, :], av[:, ds((g * 2 + k) * K, K), :]).then_inc(a_in[k], 16)

            @block.tensor
            def _(pe):
                for k in range(2):
                    pe.sem_inc(hot_free[k], 1)
                    pe.sem_inc(g_free[k], 1)
                with pe.Fori(0, ES // (2 * K)) as g:
                    for k in range(2):
                        hold(pe, hot[k], g + 1, pace["pe"])
                        for m in range(K):
                            if AD is not None:
                                hold(pe, w_ready[k], g * K + m + 1, pace["pe"])
                            else:
                                hold(pe, g_in[k][m], g * 16 + 16, pace["pe"])
                            hold(pe, pfree[m], g * 2 + k + 1, pace["pe"])
                            for c in range(KD):
                                last = nc.tensor.matmul(pA[m][:, c * P:(c + 1) * P], G2[k][m][:, c * 128:(c + 1) * 128],
                                                        HOT[k][:, m, :], start=True, stop=True)
                            last.then_inc(prod[m], 1)
                        hold(pe, prod[K - 1], g * 2 + k + 1, pace["pe"])
                        pe.sem_inc(hot_free[k], 1)
                        if AD is None:
                            pe.sem_inc(g_free[k], 1)

            @block.vector
            def _(dve):
                for k in range(2):
                    dve.sem_inc(a_free[k], 1)
                for m in range(K):
                    dve.sem_inc(pfree[m], 1)
                nc.vector.memset(ACC[:, :], 0.0)
                regs = [dve.alloc_register(f"base_{tag}{m}") for m in range(K)]
                acc = ACC[:, :].rearrange("p (c r) -> p c r", c=KD)
                with dve.Fori(0, ES // (2 * K)) as g:
                    for k in range(2):
                        t = (g * 2 + k) * K
                        hold(dve, hot_free[k], g + 1, pace["dve"])
                        nc.vector.tensor_tensor(HOT[k][:, :, :], iota[0:P, 0:P].unsqueeze(1).to_broadcast([P, K, P]),
                                                RELT[:, ds(t, K)].unsqueeze(2).to_broadcast([P, K, P]),
                                                ALU.is_equal).then_inc(hot[k], 1)
                        if AD is not None:
                            hold(dve, a_in[k], g * 16 + 16, pace["dve"])
                            for m in range(K):
                                hold(dve, g_in[k][m], g * 16 + 16, pace["dve"])
                                nc.vector.tensor_tensor(
                                    G2[k][m][:, :].rearrange("p (h d) -> p h d", d=HD),
                                    G[k][m][:, :].rearrange("p (h d) -> p h d", d=HD),
                                    AT[k][:, m, :].unsqueeze(2).to_broadcast([P, H0, HD]), ALU.mult).then_inc(w_ready[k], 1)
                            hold(dve, w_ready[k], (g + 1) * K, pace["dve"])
                            dve.sem_inc(a_free[k], 1)
                            dve.sem_inc(g_free[k], 1)
                        dve.load(regs, BASEI[0:1, ds(t, K)])
                        for m in range(K):
                            hold(dve, prod[m], g * 2 + k + 1, pace["dve"])
                            r = dve.snap(regs[m], min_val=0, max_val=N - 1)
                            nc.vector.tensor_tensor(acc[:, :, ds(r, P)], acc[:, :, ds(r, P)],
                                                    pA[m][:, 0:2 * P].rearrange("p (c r) -> p c r", c=KD),
                                                    ALU.add).then_inc(pfree[m], 1)
                            dve.drain()


def rank_rows(nc, sb, ps, sem, sems, pace, tag, ident, weight, ACC, RSUMD):
    K = 5
    with ExitStack() as s:
        col = [sb(s, f"col{tag}{k}", [128, KD * P]) for k in range(K)]
        row = [sb(s, f"rrow{tag}{k}", [P, D]) for k in range(K)]
        pT = [ps(s, f"pRT{tag}{k}", [128, 512]) for k in range(K)]
        W = sb(s, f"RWT{tag}", [128, KD, D])
        w_in = sem(f"rank_w_in_{tag}")
        c_ready, t_ready, r_ready, r_out = (sems(f"col_ready_{tag}", K), sems(f"rank_T_{tag}", K),
                                            sems(f"rrow_ready_{tag}", K), sems(f"rrow_out_{tag}", K))
        with nc.Block() as block:
            @block.scalar
            def _(act):
                v = ACC[:, :].rearrange("p (c r) -> p c r", c=KD)
                for k in range(K):
                    act.sem_inc(t_ready[k], 1)
                with act.Fori(0, NT // K) as g:
                    for k in range(K):
                        hold(act, t_ready[k], g + 1, pace["act"])
                        nc.scalar.activation(col[k][:, :].rearrange("p (c r) -> p c r", c=KD),
                                             v[:, :, ds((g * K + k) * P, P)], ACT.Copy).then_inc(c_ready[k], 1)

            @block.tensor
            def _(pe):
                if weight is not None:
                    pe.wait_ge(w_in, 16)
                with pe.Fori(0, NT // K) as g:
                    for k in range(K):
                        hold(pe, c_ready[k], g + 1, pace["pe"])
                        hold(pe, r_ready[k], g + 1, pace["pe"])
                        for c in range(KD):
                            if weight is None:
                                last = nc.tensor.transpose(pT[k][0:P, c * 128:(c + 1) * 128], col[k][:, c * P:(c + 1) * P],
                                                           ident[:, :])
                            else:
                                last = nc.tensor.matmul(pT[k][0:P, 0:D], col[k][:, c * P:(c + 1) * P], W[:, c, :],
                                                        start=(c == 0), stop=(c == KD - 1))
                        last.then_inc(t_ready[k], 1)

            @block.vector
            def _(dve):
                for k in range(K):
                    dve.sem_inc(r_ready[k], 1)
                with dve.Fori(0, NT // K) as g:
                    for k in range(K):
                        hold(dve, t_ready[k], g + 2, pace["dve"])
                        hold(dve, r_out[k], g * 16 + 16, pace["dve"])
                        nc.vector.tensor_copy(row[k][:, :], pT[k][0:P, 0:D]).then_inc(r_ready[k], 1)

            @block.sync
            def _(sp):
                if weight is not None:
                    sp.dma_start(W[:, :, :], weight.rearrange("(k p) n -> p k n", p=128)).then_inc(w_in, 16)
                for k in range(K):
                    sp.sem_inc(r_out[k], 16)
                with sp.Fori(0, NT // K) as g:
                    for k in range(K):
                        hold(sp, r_ready[k], g + 2, pace["sp"])
                        sp.dma_start(RSUMD[ds((g * K + k) * P, P), :], row[k][:, :]).then_inc(r_out[k], 16)
                for k in range(K):
                    sp.wait_ge(r_out[k], 16 * (NT // K + 1))


def add_attention(nc, sb, sem, sems, pace, RSUMD, RANKI, bias, X):
    K = 5
    b_in = sem("bias_in")
    with ExitStack() as s:
        Y = [sb(s, f"Y{k}", [P, K * D]) for k in range(2)]
        idx = [sb(s, f"yidx{k}", [P, K], i32) for k in range(2)]
        BI = sb(s, "BI", [P, D])
        y_in, y_free, idx_ready = sem.gather("y_in", 2), sems("y_free", 2), sems("yidx_ready", 2)
        with nc.Block() as block:
            @block.sync
            def _(sp):
                sp.dma_start(BI[:, :], bias.rearrange("h d -> (h d)").partition_broadcast(P)).then_inc(b_in, 16)
                sp.wait_ge(b_in, 16)

            @block.gpsimd
            def _(pool):
                with pool.Fori(0, NT // (2 * K)) as g:
                    for k in range(2):
                        hold(pool, y_free[k], g + 1, pace["pool"])
                        nc.gpsimd.memset(Y[k][:, :], 0.0).then_inc(idx_ready[k], 1)
                        nc.gpsimd.tensor_copy(idx[k][:, :], RANKI[:, ds((g * 2 + k) * K, K)]).then_inc(idx_ready[k], 1)
                        hold(pool, idx_ready[k], g * 2 + 2, pace["pool"])
                        for m in range(K):
                            pool.indirect_dma_start(Y[k][:, m * D:(m + 1) * D], None, RSUMD[:, :],
                                                    bass.IndirectOffsetOnAxis(ap=idx[k][:, m:m + 1], axis=0),
                                                    bounds_check=N - 1, oob_is_err=False).then_inc(y_in[k], 16)

            @block.vector
            def _(dve):
                for k in range(2):
                    dve.sem_inc(y_free[k], 1)
                dve.wait_ge(b_in, 16)
                with dve.Fori(0, NT // (2 * K)) as g:
                    for k in range(2):
                        hold(dve, y_in[k], g * (16 * K) + 16 * K, pace["dve"])
                        nc.vector.tensor_tensor(Y[k][:, :].rearrange("p (m d) -> p m d", d=D),
                                                Y[k][:, :].rearrange("p (m d) -> p m d", d=D),
                                                BI[:, :].unsqueeze(1).to_broadcast([P, K, D]), ALU.add)
                        dve.drain()
                        v = X[:, ds((g * 2 + k) * (K * D), K * D)]
                        nc.vector.tensor_tensor(v, v, Y[k][:, :], ALU.add)
                        dve.drain()
                        dve.sem_inc(y_free[k], 1)


def store_normed(nc, sb, sem, sems, pace, X, MEAN, RSTD, XND):
    with ExitStack() as s:
        row = [sb(s, f"nrow{k}", [P, D]) for k in range(2)]
        n_ready, n_out = sems("nrow_ready", 2), sems("nrow_out", 2)
        xv = XND.rearrange("(p i) d -> p i d", i=NT)
        with nc.Block() as block:
            @block.vector
            def _(dve):
                with dve.Fori(0, NT // 2) as g:
                    for k in range(2):
                        hold(dve, n_out[k], g * 16 + 16, pace["dve"])
                        i = g * 2 + k
                        nc.vector.tensor_scalar(row[k][:, :], X[:, ds(i * D, D)], MEAN[:, ds(i, 1)],
                                                RSTD[:, ds(i, 1)], ALU.subtract, ALU.mult).then_inc(n_ready[k], 1)

            @block.sync
            def _(sp):
                for k in range(2):
                    sp.sem_inc(n_out[k], 16)
                with sp.Fori(0, NT // 2) as g:
                    for k in range(2):
                        hold(sp, n_ready[k], g + 1, pace["sp"])
                        sp.dma_start(xv[:, ds(g * 2 + k, 1), :].rearrange("p o d -> p (o d)"),
                                     row[k][:, :]).then_inc(n_out[k], 16)
                for k in range(2):
                    sp.wait_ge(n_out[k], 16 * (NT // 2 + 1))


def gated_experts(nc, sb, ps, sem, sems, pace, sW1, sb1, sW2, sb2, sW3, sb3, eW1, eb1, eW2, eb2, eW3, eb3, gW, gb,
                  X, MEAN, RSTD, ident, ones):
    NB = NG * EH2 // 128
    with ExitStack() as s:
        w_in, w_set, w_pad = sem("ffn_w_in"), sem("ffn_w_set"), sem("ffn_w_pad")
        S1 = sb(s, "S1", [128, KD, SH1])
        S2 = sb(s, "S2", [128, KD, SH2])
        S3 = sb(s, "S3", [128, D])
        E1 = sb(s, "E1", [128, KD, NG, EH1])
        E2 = sb(s, "E2", [128, NG, 128])
        E3 = sb(s, "E3", [128, NB, D])
        EB3 = sb(s, "EB3", [NG, D])
        SB3 = sb(s, "SB3", [1, D])
        GW = sb(s, "GW", [128, KD, NG])
        GB = sb(s, "GB", [1, NG])
        B1 = sb(s, "B1s", [128, KD])
        B2 = sb(s, "B2s", [128, 1])
        C1 = sb(s, "C1", [128, NG])
        C2 = sb(s, "C2", [128, NB])
        SEL = sb(s, "SEL", [NG, NB, 128])
        xn = [sb(s, f"fxn{k}", [P, D]) for k in range(GT)]
        xT = [sb(s, f"fxT{k}", [128, KD, GC]) for k in range(2)]
        h1 = sb(s, "h1", [128, KD, GC])
        h2 = sb(s, "h2", [128, GC])
        e1 = sb(s, "e1", [128, NG, GC])
        e2 = sb(s, "e2", [128, NB, GC])
        e2w = sb(s, "e2w", [128, NB, GC])
        wT = [sb(s, f"wT{k}", [NG, GC]) for k in range(2)]
        g_ = {n: sb(s, f"gate_{n}", [P, GT, NG]) for n in ("l", "p", "eq", "m1", "q", "w")}
        r_ = {n: sb(s, f"gred_{n}", [P, GT]) for n in ("mx", "sum", "v1", "v2", "d", "e", "f", "t")}
        pT = ps(s, "fpT", [128, 512])
        pG = ps(s, "fpG", [128, 512])
        pW = ps(s, "fpW", [128, 512])
        pM = [ps(s, f"fpM{k}", [128, 512]) for k in range(3)]
        pO = [ps(s, f"fpO{k}", [128, 512]) for k in range(GT)]
        xn_ready, t_ready, x_ready = sem("fxn_ready"), sem("fxT_psum"), sem("fxT_ready")
        l_ready, w_ready, wt_ready, wt_copied, wb_ready, ex_ready, gx_ready = (
            sem("glogits"), sem("gweights"), sem("gwT"), sem("gwT_copied"), sem("gw_spread"), sem("gexp"), sem("gexp_in"))
        e2_ready, e2w_ready, o_ready, x_done = sem("e2_ready"), sem("e2w_ready"), sems("fout", GT), sem("x_updated")
        o_read, l_read = sems("fout_read", GT), sem("glogits_read")
        m_ready = sems("fmid", 3)
        m_read = sems("fmid_read", 3)
        NM = KD + 1 + NG + NB
        bank = [n % 3 for n in range(NM)]
        per = [bank.count(b) for b in range(3)]
        with nc.Block() as block:
            @block.sync
            def _(sp):
                loads = [
                    (S1[:, :, :], sW1.rearrange("(k p) n -> p k n", p=128)),
                    (S2[:, :, :], sW2.rearrange("(k p) n -> p k n", p=128)),
                    (S3[:, :], sW3[:, :]),
                    (EB3[:, :], eb3[:, :]), (SB3[:, :], sb3.rearrange("(o n) -> o n", o=1)),
                    (GW[:, :, :], gW.rearrange("(k p) n -> p k n", p=128)), (GB[:, :], gb.rearrange("(o n) -> o n", o=1)),
                    (B1[:, :], sb1.rearrange("(k p) -> p k", p=128)), (B2[:, :], sb2.rearrange("(p o) -> p o", o=1)),
                    (C1[:, :], eb1.rearrange("e p -> p e")),
                ]
                for k in range(KD):
                    loads.append((E1[:, k, :, :], eW1[:, k * 128:(k + 1) * 128, :].rearrange("e p n -> p e n")))
                for b in range(NB):
                    for h in range(2):
                        a = slice(h * EH2, (h + 1) * EH2)
                        loads.append((E3[a, b, :], eW3[2 * b + h, :, :]))
                        loads.append((C2[a, b:b + 1], eb2[2 * b + h, :].rearrange("(p o) -> p o", o=1)))
                sp.wait_ge(w_set, 1)
                for e in range(NG):
                    a = (e % 2) * EH2
                    loads.append((E2[:, e, a:a + EH2], eW2[e, :, :]))
                for to, of in loads:
                    sp.dma_start(to, of, allow_slow_non_contiguous=True).then_inc(w_in, 16)
                sp.wait_ge(w_in, 16 * len(loads))

            @block.gpsimd
            def _(pool):
                nc.gpsimd.memset(E2[:, :, :], 0.0).then_inc(w_set, 1)
                nc.gpsimd.memset(SEL[:, :, :], 1.0).then_inc(w_pad, 1)
                pool.wait_ge(w_pad, 1)
                nc.gpsimd.affine_select(out=SEL[:, :, :], in_=SEL[:, :, :], compare_op=ALU.is_ge, fill=0.0, base=0,
                                        pattern=[[128, NB], [1, 128]], channel_multiplier=-EH2).then_inc(w_pad, 1)
                pool.wait_ge(w_pad, 2)
                nc.gpsimd.affine_select(out=SEL[:, :, :], in_=SEL[:, :, :], compare_op=ALU.is_ge, fill=0.0, base=EH2 - 1,
                                        pattern=[[-128, NB], [-1, 128]], channel_multiplier=EH2)

        NGR = NT // GT
        with nc.Block() as block:
            @block.vector
            def _(dve):
                def spread(v):
                    return v[:, :].unsqueeze(2).to_broadcast([P, GT, NG])

                def first_max(v, top, mark):
                    nc.vector.tensor_reduce(r_[top][:, :], v[:, :, :], AX.X, ALU.max)
                    dve.drain()
                    nc.vector.tensor_tensor(g_["eq"][:, :, :], v[:, :, :], spread(r_[top]), ALU.is_equal)
                    nc.vector.memset(r_["t"][:, :], 1.0)
                    dve.drain()
                    for e in range(NG):
                        nc.vector.tensor_tensor(mark[:, :, e], g_["eq"][:, :, e], r_["t"][:, :], ALU.mult)
                        dve.drain()
                        if e < NG - 1:
                            nc.vector.tensor_tensor(r_["t"][:, :], r_["t"][:, :], mark[:, :, e], ALU.subtract)
                            dve.drain()

                def normed(g):
                    for m in range(GT):
                        i = g * GT + m
                        nc.vector.tensor_scalar(xn[m][:, :], X[:, ds(i * D, D)], MEAN[:, ds(i, 1)],
                                                RSTD[:, ds(i, 1)], ALU.subtract, ALU.mult).then_inc(xn_ready, 1)

                def gates(g):
                    hold(dve, l_ready, g + 1, pace["dve"])
                    nc.vector.tensor_copy(g_["l"][:, :, :],
                                          pG[0:P, 0:GT * NG].rearrange("p (k e) -> p k e", e=NG)).then_inc(l_read, 1)
                    dve.drain()
                    nc.vector.tensor_reduce(r_["mx"][:, :], g_["l"][:, :, :], AX.X, ALU.max)
                    dve.drain()
                    nc.vector.tensor_tensor(g_["l"][:, :, :], g_["l"][:, :, :], spread(r_["mx"]),
                                            ALU.subtract).then_inc(gx_ready, 1)
                    hold(dve, ex_ready, g * 2 + 1, pace["dve"])
                    nc.vector.tensor_reduce(r_["sum"][:, :], g_["p"][:, :, :], AX.X, ALU.add)
                    dve.drain()
                    nc.vector.reciprocal(r_["sum"][:, :], r_["sum"][:, :])
                    dve.drain()
                    nc.vector.tensor_tensor(g_["p"][:, :, :], g_["p"][:, :, :], spread(r_["sum"]), ALU.mult)
                    dve.drain()
                    first_max(g_["p"], "v1", g_["m1"])
                    nc.vector.scalar_tensor_tensor(g_["q"][:, :, :], g_["m1"][:, :, :], -4.0, g_["p"][:, :, :],
                                                   ALU.mult, ALU.add)
                    dve.drain()
                    first_max(g_["q"], "v2", g_["w"])
                    nc.vector.tensor_tensor(r_["d"][:, :], r_["v2"][:, :], r_["v1"][:, :], ALU.subtract).then_inc(gx_ready, 1)

                def weigh(g, k):
                    hold(dve, ex_ready, g * 2 + 2, pace["dve"])
                    nc.vector.tensor_scalar(r_["f"][:, :], r_["e"][:, :], 1.0, None, ALU.add)
                    nc.vector.tensor_tensor(g_["w"][:, :, :], g_["w"][:, :, :], spread(r_["e"]), ALU.mult)
                    dve.drain()
                    nc.vector.reciprocal(r_["f"][:, :], r_["f"][:, :])
                    nc.vector.tensor_tensor(g_["w"][:, :, :], g_["w"][:, :, :], g_["m1"][:, :, :], ALU.add)
                    dve.drain()
                    nc.vector.tensor_tensor(g_["w"][:, :, :], g_["w"][:, :, :], spread(r_["f"]), ALU.mult).then_inc(w_ready, 1)
                    hold(dve, wt_ready, g + 1, pace["dve"])
                    nc.vector.tensor_copy(wT[k][:, :], pG[0:NG, 256:256 + GC]).then_inc(wt_copied, 1)

                def first(g, k):
                    normed(g)
                    gates(g)

                def rest(g, k, more):
                    if more:
                        normed(g + 1)
                    weigh(g, k)
                    hold(dve, wb_ready, g + 1, pace["dve"])
                    hold(dve, e2_ready, g + 1, pace["dve"])
                    nc.vector.tensor_tensor(e2w[:, :, :], e2[:, :, :],
                                            pW[:, 0:NB * GC].rearrange("p (b c) -> p b c", c=GC), ALU.mult).then_inc(e2w_ready, 1)
                    if more:
                        gates(g + 1)
                    for m in range(GT):
                        hold(dve, o_ready[m], g + 1, pace["dve"])
                        v = X[:, ds((g * GT + m) * D, D)]
                        nc.vector.tensor_tensor(v, v, pO[m][0:P, 0:D], ALU.add).then_inc(o_read[m], 1)

                alternate(dve, NGR, first, rest)

            @block.scalar
            def _(act):
                def normed(g, k):
                    hold(act, t_ready, g + 1, pace["act"])
                    nc.scalar.activation(xT[k][:, :, :].rearrange("p c (k q) -> p k c q", q=P),
                                         pT[:, 0:GT * KD * P].rearrange("p (k c q) -> p k c q", c=KD, q=P),
                                         ACT.Copy).then_inc(x_ready, 1)

                def exp_gates(g):
                    hold(act, gx_ready, g * 2 + 1, pace["act"])
                    nc.scalar.activation(g_["p"][:, :, :], g_["l"][:, :, :], ACT.Exp).then_inc(ex_ready, 1)

                def exp_second(g):
                    hold(act, gx_ready, g * 2 + 2, pace["act"])
                    nc.scalar.activation(r_["e"][:, :], r_["d"][:, :], ACT.Exp).then_inc(ex_ready, 1)

                def first(g, k):
                    normed(g, k)
                    exp_gates(g)

                def rest(g, k, more):
                    def mid(n, to, b):
                        hold(act, m_ready[bank[n]], g * per[bank[n]] + n // 3 + 1, pace["act"])
                        nc.scalar.activation(to, pM[bank[n]][:, 0:GC], ACT.Relu, bias=b).then_inc(m_read[bank[n]], 1)

                    for n in range(KD):
                        mid(n, h1[:, n, :], B1[:, n:n + 1])
                    for e in range(NG):
                        mid(KD + e, e1[:, e, :], C1[:, e:e + 1])
                        if e == 1:
                            exp_second(g)
                    if more:
                        normed(g + 1, 1 - k)
                    mid(KD + NG, h2[:, :], B2[:, :])
                    for b in range(NB):
                        mid(KD + NG + 1 + b, e2[:, b, :], C2[:, b:b + 1])
                    hold(act, m_read[bank[NM - 1]], (g + 1) * per[bank[NM - 1]] + 1, pace["act"])
                    act.sem_inc(e2_ready, 1)
                    if more:
                        exp_gates(g + 1)

                alternate(act, NGR, first, rest)

            @block.tensor
            def _(pe):
                for b in range(3):
                    pe.sem_inc(m_read[b], 1)
                for m in range(GT):
                    pe.sem_inc(o_read[m], 1)
                pe.sem_inc(l_read, 1)
                pe.sem_inc(wt_copied, 1)

                def turn(g):
                    hold(pe, xn_ready, g * GT + GT, pace["pe"])
                    for m in range(GT):
                        for c in range(KD):
                            last = nc.tensor.transpose(pT[:, (m * KD + c) * P:(m * KD + c + 1) * P],
                                                       xn[m][:, c * 128:(c + 1) * 128], ident[0:P, 0:P])
                    last.then_inc(t_ready, 1)

                def logits(g, k):
                    hold(pe, x_ready, g + 1, pace["pe"])
                    hold(pe, wt_copied, g + 1, pace["pe"])
                    for m in range(GT):
                        o = pG[0:P, m * NG:(m + 1) * NG]
                        for c in range(KD):
                            nc.tensor.matmul(o, xT[k][:, c, m * P:(m + 1) * P], GW[:, c, :], start=(c == 0), stop=False)
                        last = nc.tensor.matmul(o, ones[:, 0:P], GB[:, :], start=False, stop=True)
                    last.then_inc(l_ready, 1)

                def weights(g):
                    hold(pe, w_ready, g + 1, pace["pe"])
                    for m in range(GT):
                        last = nc.tensor.transpose(pG[0:NG, 256 + m * P:256 + (m + 1) * P], g_["w"][:, m, :], ident[0:P, 0:P])
                    last.then_inc(wt_ready, 1)

                def first(g, k):
                    turn(g)
                    logits(g, k)

                def rest(g, k, more):
                    def mid(n, pairs):
                        hold(pe, m_read[bank[n]], g * per[bank[n]] + n // 3 + 1, pace["pe"])
                        for c, (w, v) in enumerate(pairs):
                            last = nc.tensor.matmul(pM[bank[n]][:, 0:GC], w, v, start=(c == 0), stop=(c == len(pairs) - 1))
                        last.then_inc(m_ready[bank[n]], 1)

                    for n in range(KD):
                        mid(n, [(S1[:, c, n * 128:(n + 1) * 128], xT[k][:, c, :]) for c in range(KD)])
                    for e in range(NG):
                        mid(KD + e, [(E1[:, c, e, :], xT[k][:, c, :]) for c in range(KD)])
                    weights(g)
                    if more:
                        turn(g + 1)
                    for b in range(3):
                        n = max(n for n in range(KD + NG) if bank[n] == b)
                        hold(pe, m_read[b], g * per[b] + n // 3 + 2, pace["pe"])
                    mid(KD + NG, [(S2[:, c, :], h1[:, c, :]) for c in range(KD)])
                    for b in range(NB):
                        mid(KD + NG + 1 + b, [(E2[:, 2 * b + h, :], e1[:, 2 * b + h, :]) for h in range(2)])
                    hold(pe, wt_copied, g + 2, pace["pe"])
                    for b in range(NB):
                        last = nc.tensor.matmul(pW[:, b * GC:(b + 1) * GC], SEL[:, b, :], wT[k][:, :], start=True, stop=True)
                    last.then_inc(wb_ready, 1)
                    if more:
                        logits(g + 1, 1 - k)
                    hold(pe, m_read[bank[KD + NG]], g * per[bank[KD + NG]] + (KD + NG) // 3 + 2, pace["pe"])
                    for m in range(GT):
                        hold(pe, o_read[m], g + 1, pace["pe"])
                        o = pO[m][0:P, 0:D]
                        a = slice(m * P, (m + 1) * P)
                        nc.tensor.matmul(o, h2[:, a], S3[:, :], start=True, stop=False)
                        nc.tensor.matmul(o, wT[k][:, a], EB3[:, :], start=False, stop=False)
                        nc.tensor.matmul(o, ones[:, 0:P], SB3[:, :], start=False, stop=False)
                    hold(pe, e2w_ready, g + 1, pace["pe"])
                    for m in range(GT):
                        a = slice(m * P, (m + 1) * P)
                        for b in range(NB):
                            last = nc.tensor.matmul(pO[m][0:P, 0:D], e2w[:, b, a], E3[:, b, :], start=False, stop=(b == NB - 1))
                        last.then_inc(o_ready[m], 1)

                alternate(pe, NGR, first, rest)


def mean_layer(nc, sb, ps, sem, sems, pace, RSUMD, RANKI, RDEG, gamma, beta, X, MEAN, RSTD, ident, epsc):
    K = 5
    with ExitStack() as s:
        GA = sb(s, "GA", [128, KD])
        BE = sb(s, "BE", [128, KD])
        Z = sb(s, "Z", [128, KD, N])
        BST = sb(s, "BST", [128, KD, NT, 6])
        BMV = sb(s, "BMV", [128, KD, 2])
        SC = sb(s, "SC", [128, KD])
        SH = sb(s, "SH", [128, KD])
        Y = [sb(s, f"mY{k}", [P, K * D]) for k in range(2)]
        idx = [sb(s, f"midx{k}", [P, K], i32) for k in range(2)]
        xn = [sb(s, f"mxn{k}", [P, D]) for k in range(K)]
        z = [sb(s, f"mz{k}", [P, D]) for k in range(K)]
        zr = [sb(s, f"zr{k}", [128, KD, P]) for k in range(K)]
        pT = [ps(s, f"mpT{k}", [128, 512]) for k in range(K)]
        w_in, y_in, y_free, idx_ready = sem("bn_w_in"), sem.gather("my_in", 2), sems("my_free", 2), sems("midx_ready", 2)
        x_ready, z_ready, t_ready, b_read = (sems("mxn_ready", K), sems("mz_ready", K), sems("mz_T", K),
                                             sems("mz_copied", K))
        with nc.Block() as block:
            @block.sync
            def _(sp):
                sp.dma_start(GA[:, :], gamma.rearrange("(k p) -> p k", p=128), allow_slow_non_contiguous=True).then_inc(w_in, 16)
                sp.dma_start(BE[:, :], beta.rearrange("(k p) -> p k", p=128), allow_slow_non_contiguous=True).then_inc(w_in, 16)
                sp.wait_ge(w_in, 32)

            @block.gpsimd
            def _(pool):
                with pool.Fori(0, NT // (2 * K)) as g:
                    for k in range(2):
                        hold(pool, y_free[k], g + 1, pace["pool"])
                        nc.gpsimd.memset(Y[k][:, :], 0.0).then_inc(idx_ready[k], 1)
                        nc.gpsimd.tensor_copy(idx[k][:, :], RANKI[:, ds((g * 2 + k) * K, K)]).then_inc(idx_ready[k], 1)
                        hold(pool, idx_ready[k], g * 2 + 2, pace["pool"])
                        for m in range(K):
                            pool.indirect_dma_start(Y[k][:, m * D:(m + 1) * D], None, RSUMD[:, :],
                                                    bass.IndirectOffsetOnAxis(ap=idx[k][:, m:m + 1], axis=0),
                                                    bounds_check=N - 1, oob_is_err=False).then_inc(y_in[k], 16)

            @block.vector
            def _(dve):
                for k in range(2):
                    dve.sem_inc(y_free[k], 1)
                with dve.Fori(0, NT // (2 * K)) as g:
                    for k in range(2):
                        c5 = g * 2 + k
                        for m in range(K):
                            nc.vector.tensor_scalar(xn[m][:, :], X[:, ds((c5 * K + m) * D, D)], MEAN[:, ds(c5 * K + m, 1)],
                                                    RSTD[:, ds(c5 * K + m, 1)], ALU.subtract, ALU.mult).then_inc(x_ready[m], 1)
                        hold(dve, y_in[k], g * (16 * K) + 16 * K, pace["dve"])
                        for m in range(K):
                            hold(dve, x_ready[m], c5 + 1, pace["dve"])
                            nc.vector.scalar_tensor_tensor(z[m][:, :], Y[k][:, m * D:(m + 1) * D], RDEG[:, ds(c5 * K + m, 1)],
                                                           xn[m][:, :], ALU.mult, ALU.add).then_inc(z_ready[m], 1)
                        hold(dve, z_ready[K - 1], c5 + 1, pace["dve"])
                        dve.sem_inc(y_free[k], 1)
                        for m in range(K):
                            hold(dve, b_read[m], c5 + 2, pace["dve"])
                            for c in range(KD):
                                nc.vector.bn_stats(BST[:, c, ds(c5 * K + m, 1), :].rearrange("p o f -> p (o f)"),
                                                   Z[:, c, ds((c5 * K + m) * P, P)])

            @block.scalar
            def _(act):
                with act.Fori(0, NT // K) as g:
                    for m in range(K):
                        hold(act, t_ready[m], g + 1, pace["act"])
                        nc.scalar.activation(Z[:, :, ds((g * K + m) * P, P)],
                                             pT[m][:, 0:2 * P].rearrange("p (c q) -> p c q", c=KD), ACT.Copy).then_inc(b_read[m], 1)

            @block.tensor
            def _(pe):
                for m in range(K):
                    pe.sem_inc(b_read[m], 1)
                with pe.Fori(0, NT // K) as g:
                    for m in range(K):
                        hold(pe, z_ready[m], g + 1, pace["pe"])
                        hold(pe, b_read[m], g + 1, pace["pe"])
                        for c in range(KD):
                            last = nc.tensor.transpose(pT[m][:, c * P:(c + 1) * P], z[m][:, c * 128:(c + 1) * 128],
                                                       ident[0:P, 0:P])
                        last.then_inc(t_ready[m], 1)

        agg, sq = sem("bn_agg"), sem("bn_sqrt")
        with nc.Block() as block:
            @block.vector
            def _(dve):
                for c in range(KD):
                    nc.vector.bn_aggr(BMV[:, c, :], BST[:, c, :, :].rearrange("p g f -> p (g f)"))
                dve.drain()
                nc.vector.tensor_copy(SH[:, :], BMV[:, :, 1]).then_inc(agg, 1)
                dve.wait_ge(sq, 1)
                nc.vector.reciprocal(SC[:, :], SC[:, :])
                dve.drain()
                nc.vector.tensor_tensor(SC[:, :], SC[:, :], GA[:, :], ALU.mult)
                dve.drain()
                nc.vector.tensor_tensor(SH[:, :], BMV[:, :, 0], SC[:, :], ALU.mult)
                dve.drain()
                nc.vector.tensor_tensor(SH[:, :], BE[:, :], SH[:, :], ALU.subtract)

            @block.scalar
            def _(act):
                act.wait_ge(agg, 1)
                nc.scalar.activation(SC[:, :], SH[:, :], ACT.Sqrt, bias=epsc[:, :]).then_inc(sq, 1)

        zr_ready, zt_ready, zx_done = sems("zr_ready", K), sems("zT_psum", K), sems("z_added", K)
        with nc.Block() as block:
            @block.scalar
            def _(act):
                for m in range(K):
                    act.sem_inc(zt_ready[m], 1)
                with act.Fori(0, NT // K) as g:
                    for m in range(K):
                        hold(act, zt_ready[m], g + 1, pace["act"])
                        for c in range(KD):
                            last = nc.scalar.activation(zr[m][:, c, :], Z[:, c, ds((g * K + m) * P, P)], ACT.Relu,
                                                        bias=SH[:, c:c + 1], scale=SC[:, c:c + 1])
                        last.then_inc(zr_ready[m], 1)

            @block.tensor
            def _(pe):
                for m in range(K):
                    pe.sem_inc(zx_done[m], 1)
                with pe.Fori(0, NT // K) as g:
                    for m in range(K):
                        hold(pe, zr_ready[m], g + 1, pace["pe"])
                        hold(pe, zx_done[m], g + 1, pace["pe"])
                        for c in range(KD):
                            last = nc.tensor.transpose(pT[m][0:P, c * 128:(c + 1) * 128], zr[m][:, c, :], ident[:, :])
                        last.then_inc(zt_ready[m], 1)

            @block.vector
            def _(dve):
                with dve.Fori(0, NT // K) as g:
                    for m in range(K):
                        hold(dve, zt_ready[m], g + 2, pace["dve"])
                        v = X[:, ds((g * K + m) * D, D)]
                        nc.vector.tensor_tensor(v, v, pT[m][0:P, 0:D], ALU.add).then_inc(zx_done[m], 1)


def top_experts(nc, sb, ps, sem, sems, pace, router_w, router_b, W1, b1, W2, b2, X, MEAN, RSTD, ident, iota, ones, out):
    with ExitStack() as s:
        M1 = sb(s, "M1", [128, KD, NE * EH])
        M2 = sb(s, "M2", [128, HB, D])
        RWN = sb(s, "RWN", [NE, D])
        RW = sb(s, "RW", [128, KD, NE])
        RB = sb(s, "RB", [1, NE])
        MB1 = sb(s, "MB1", [128, HB])
        MB2 = sb(s, "MB2", [NE, D])
        OFFM = sb(s, "OFFM", [NE, NE, EH], bf16)
        xn = [sb(s, f"txn{k}", [P, D]) for k in range(GT)]
        xT = [sb(s, f"txT{k}", [128, KD, GC]) for k in range(2)]
        LG = sb(s, "LG", [P, GT, NE])
        T8 = sb(s, "T8", [P, GT, 8])
        I8 = sb(s, "I8", [P, GT, 8], u32)
        IF = sb(s, "IF", [P, GT])
        OH = sb(s, "OH", [P, GT, NE])
        OT = [sb(s, f"OT{k}", [NE, GC]) for k in range(2)]
        OTB = [sb(s, f"OTB{k}", [NE, GC], bf16) for k in range(2)]
        hid = sb(s, "hid", [128, HB, GC])
        O = [sb(s, f"O{k}", [P, D]) for k in range(GT)]
        pT = ps(s, "tpT", [128, 512])
        pL = ps(s, "tpL", [128, 512])
        pH = [ps(s, f"tpH{k}", [128, 512]) for k in range(4)]
        NGR = NT // GT
        pO = [ps(s, f"tpO{k}", [128, 512]) for k in range(GT)]
        w_in, o_set, rt, rc = sem("tw_in"), sem("offm_set"), sem("router_T"), sem("router_copied")
        xn_ready, t_ready, x_ready, l_ready, oh_ready, ot_ready, ot_copied = (
            sem("txn_ready"), sem("txT_psum"), sem("txT_ready"), sem("logits"), sem("onehot_ready"), sem("onehot_T"),
            sem("onehot_Tcopied"))
        h_ready, h_read = sems("hid_psum", 4), sems("hid_read", 4)
        o_ready, O_ready, O_out = sems("tout", GT), sems("O_ready", GT), sems("O_out", GT)
        with nc.Block() as block:
            @block.sync
            def _(sp):
                n = 0
                for k in range(KD):
                    for q in range(4):
                        a = slice(q * NE // 4, (q + 1) * NE // 4)
                        sp.dma_start(M1[:, k, :].rearrange("p (e h) -> p e h", h=EH)[:, a, :],
                                     W1[a, k * 128:(k + 1) * 128, :].rearrange("e p h -> p e h")).then_inc(w_in, 16)
                        n += 16
                sp.dma_start(M2[:, :, :],
                             W2.rearrange("e h d -> (e h) d").rearrange("(b q) d -> q b d", q=128)).then_inc(w_in, 16)
                sp.dma_start(MB1[:, :], b1.rearrange("e h -> (e h)").rearrange("(b q) -> q b", q=128),
                             allow_slow_non_contiguous=True).then_inc(w_in, 16)
                sp.dma_start(RWN[:, :], router_w[:, :]).then_inc(w_in, 16)
                sp.dma_start(RB[:, :], router_b.rearrange("(o e) -> o e", o=1)).then_inc(w_in, 16)
                sp.dma_start(MB2[:, :], b2[:, :]).then_inc(w_in, 16)
                n += 80
                sp.wait_ge(w_in, n)

            @block.gpsimd
            def _(pool):
                nc.gpsimd.memset(OFFM[:, :, :], LOW).then_inc(o_set, 1)
                pool.wait_ge(o_set, 1)
                nc.gpsimd.affine_select(out=OFFM[:, :, :], in_=OFFM[:, :, :], compare_op=ALU.not_equal, fill=0.0, base=0,
                                        pattern=[[-1, NE], [0, EH]], channel_multiplier=1)

            @block.tensor
            def _(pe):
                pe.wait_ge(w_in, 16 * 13)
                for c in range(KD):
                    last = nc.tensor.transpose(pT[:, c * NE:(c + 1) * NE], RWN[:, c * 128:(c + 1) * 128], ident[0:NE, 0:NE])
                last.then_inc(rt, 1)

            @block.vector
            def _(dve):
                dve.wait_ge(rt, 1)
                nc.vector.tensor_copy(RW[:, :, :], pT[:, 0:KD * NE].rearrange("p (c e) -> p c e", e=NE))

        with nc.Block() as block:
            @block.vector
            def _(dve):
                def route(g, k):
                    for m in range(GT):
                        i = g * GT + m
                        nc.vector.tensor_scalar(xn[m][:, :], X[:, ds(i * D, D)], MEAN[:, ds(i, 1)],
                                                RSTD[:, ds(i, 1)], ALU.subtract, ALU.mult).then_inc(xn_ready, 1)
                    hold(dve, l_ready, g + 1, pace["dve"])
                    nc.vector.tensor_copy(LG[:, :, :], pL[0:P, 0:GT * NE].rearrange("p (k e) -> p k e", e=NE))
                    dve.drain()
                    for m in range(GT):
                        nc.vector.max(T8[:, m, :], LG[:, m, :])
                    dve.drain()
                    for m in range(GT):
                        nc.vector.max_index(I8[:, m, :], T8[:, m, :], LG[:, m, :])
                    dve.drain()
                    nc.vector.tensor_copy(IF[:, :], I8[:, :, 0])
                    dve.drain()
                    nc.vector.tensor_tensor(OH[:, :, :], iota[0:P, 0:NE].unsqueeze(1).to_broadcast([P, GT, NE]),
                                            IF[:, :].unsqueeze(2).to_broadcast([P, GT, NE]), ALU.is_equal).then_inc(oh_ready, 1)
                    hold(dve, ot_ready, g + 1, pace["dve"])
                    nc.vector.tensor_copy(OTB[k][:, :], pL[0:NE, 256:256 + GC])
                    nc.vector.tensor_copy(OT[k][:, :], pL[0:NE, 256:256 + GC]).then_inc(ot_copied, 1)

                def rest(g, k, more):
                    if more:
                        route(g + 1, 1 - k)
                    for m in range(GT):
                        hold(dve, o_ready[m], g + 1, pace["dve"])
                        hold(dve, O_out[m], g * 16 + 16, pace["dve"])
                        nc.vector.scalar_tensor_tensor(O[m][:, :], pO[m][0:P, 0:D], 0.0, X[:, ds((g * GT + m) * D, D)],
                                                       ALU.max, ALU.add).then_inc(O_ready[m], 1)

                alternate(dve, NGR, route, rest)

            @block.scalar
            def _(act):
                def normed(g, k):
                    hold(act, t_ready, g + 1, pace["act"])
                    nc.scalar.activation(xT[k][:, :, :].rearrange("p c (k q) -> p k c q", q=P),
                                         pT[:, 0:GT * KD * P].rearrange("p (k c q) -> p k c q", c=KD, q=P),
                                         ACT.Copy).then_inc(x_ready, 1)

                def rest(g, k, more):
                    for b in range(HB):
                        if b == HB // 2 and more:
                            normed(g + 1, 1 - k)
                        hold(act, h_ready[b % 4], g * (HB // 4) + b // 4 + 1, pace["act"])
                        nc.scalar.activation(hid[:, b, :], pH[b % 4][:, 0:GC], ACT.Relu,
                                             bias=MB1[:, b:b + 1]).then_inc(h_read[b % 4], 1)

                alternate(act, NGR, normed, rest)

            @block.tensor
            def _(pe):
                for b in range(4):
                    pe.sem_inc(h_read[b], 1)
                for m in range(GT):
                    pe.sem_inc(O_ready[m], 1)

                def turn(g):
                    hold(pe, xn_ready, g * GT + GT, pace["pe"])
                    for m in range(GT):
                        for c in range(KD):
                            last = nc.tensor.transpose(pT[:, (m * KD + c) * P:(m * KD + c + 1) * P],
                                                       xn[m][:, c * 128:(c + 1) * 128], ident[0:P, 0:P])
                    last.then_inc(t_ready, 1)

                def logits(g, k):
                    hold(pe, x_ready, g + 1, pace["pe"])
                    for m in range(GT):
                        o = pL[0:P, m * NE:(m + 1) * NE]
                        for c in range(KD):
                            nc.tensor.matmul(o, xT[k][:, c, m * P:(m + 1) * P], RW[:, c, :], start=(c == 0), stop=False)
                        last = nc.tensor.matmul(o, ones[:, 0:P], RB[:, :], start=False, stop=True)
                    last.then_inc(l_ready, 1)

                def choice(g):
                    hold(pe, oh_ready, g + 1, pace["pe"])
                    for m in range(GT):
                        last = nc.tensor.transpose(pL[0:NE, 256 + m * P:256 + (m + 1) * P], OH[:, m, :], ident[0:P, 0:P])
                    last.then_inc(ot_ready, 1)

                def first(g, k):
                    turn(g)
                    logits(g, k)
                    choice(g)

                def hidden(g, k, b):
                    hold(pe, h_read[b % 4], g * (HB // 4) + b // 4 + 1, pace["pe"])
                    o = pH[b % 4][:, 0:GC]
                    nc.tensor.matmul(o, OFFM[:, 2 * b:2 * b + 2, :].rearrange("p e h -> p (e h)"), OTB[k][:, :],
                                     start=True, stop=False)
                    for c in range(KD):
                        last = nc.tensor.matmul(o, M1[:, c, b * 128:(b + 1) * 128], xT[k][:, c, :],
                                                start=False, stop=(c == KD - 1))
                    last.then_inc(h_ready[b % 4], 1)

                def rest(g, k, more):
                    hold(pe, ot_copied, g + 1, pace["pe"])
                    for b in range(HB):
                        if b == HB // 4 and more:
                            turn(g + 1)
                        if b == HB - 2 and more:
                            logits(g + 1, 1 - k)
                        hidden(g, k, b)
                    for m in range(GT):
                        a = slice(m * P, (m + 1) * P)
                        o = pO[m][0:P, 0:D]
                        if m and more:
                            choice(g + 1)
                        hold(pe, O_ready[m], g + 1, pace["pe"])
                        nc.tensor.matmul(o, OT[k][:, a], MB2[:, :], start=True, stop=False)
                        for b in range(HB):
                            if m == 0:
                                hold(pe, h_read[b % 4], g * (HB // 4) + b // 4 + 2, pace["pe"])
                            last = nc.tensor.matmul(o, hid[:, b, a], M2[:, b, :], start=False, stop=(b == HB - 1))
                        last.then_inc(o_ready[m], 1)

                alternate(pe, NGR, first, rest)

            @block.sync
            def _(sp):
                ov = out.rearrange("(p i) d -> p i d", i=NT)
                for k in range(GT):
                    sp.sem_inc(O_out[k], 16)
                with sp.Fori(0, NT // GT) as g:
                    for k in range(GT):
                        hold(sp, O_ready[k], g + 2, pace["sp"])
                        sp.dma_start(ov[:, ds(g * GT + k, 1), :].rearrange("p o d -> p (o d)"), O[k][:, :]).then_inc(O_out[k], 16)
                for k in range(GT):
                    sp.wait_ge(O_out[k], 16 * (NT // GT + 1))


_INS = ["x", "src", "dst", "edge_attr_64", "L0_gnn_W_fc", "L0_gnn_W_e", "L0_gnn_attn_h", "L0_gnn_attn_e", "L0_gnn_attn_t",
        "L0_gnn_bias", "L0_ffn_sW1", "L0_ffn_sb1", "L0_ffn_sW2", "L0_ffn_sb2", "L0_ffn_sW3", "L0_ffn_sb3", "L0_ffn_eW1",
        "L0_ffn_eb1", "L0_ffn_eW2", "L0_ffn_eb2", "L0_ffn_eW3", "L0_ffn_eb3", "L0_ffn_gW", "L0_ffn_gb", "L1_gnn_W_src",
        "L1_gnn_gamma", "L1_gnn_beta", "L1_ffn_router_w", "L1_ffn_router_b", "L1_ffn_W1", "L1_ffn_b1", "L1_ffn_W2",
        "L1_ffn_b2"]


def kernel(**inputs):
    import numpy as _np
    import concourse.bacc as _bacc
    from concourse import mybir as _mybir
    from concourse.bass_utils import run_bass_kernel_spmd as _run

    nc = _bacc.Bacc("TRN2", target_bir_lowering=False, num_devices=1)
    arrays, args = {}, []
    for name in _INS:
        a = _np.ascontiguousarray(inputs[name])
        arrays[f"in_{name}_dram"] = a
        args.append(nc.dram_tensor(f"in_{name}_dram", a.shape, _mybir.dt.from_np(a.dtype), kind="ExternalInput").ap())
    args.append(nc.dram_tensor("out_0_dram", (N, D), _mybir.dt.from_np(_np.dtype("float32")), kind="ExternalOutput").ap())
    program(nc, *args)
    r = _run(nc, [arrays], core_ids=[0])
    return r.results[0]["out_0_dram"]
```
